# Optimizing a Trainium2 kernel written in Bass

```python
import numpy as np
import jax
import jax.numpy as jnp

def _softmax(x, axis=-1):
    return jax.nn.softmax(x, axis=axis)

def _gelu(x):
    return jax.nn.gelu(x, approximate=True)

def _silu(x):
    return jax.nn.silu(x)

def _sigmoid(x):
    return jax.nn.sigmoid(x)

def _layernorm(x, axis=-1, eps=1e-05):
    m = jnp.mean(x, axis=axis, keepdims=True)
    v = jnp.var(x, axis=axis, keepdims=True)
    return (x - m) / jnp.sqrt(v + eps)

def _scatter_add(tgt, idx, src, axis=0):
    return tgt.at[idx].add(src)

def _segment_sum(src, seg, n):
    return jax.ops.segment_sum(src, seg, n)
kernel_name = 'mk_decoder_postln_d1_seqx_r4_22f595'

def setup_inputs(seed: int=0):
    np.random.seed(seed)
    _w = jnp.asarray

    def _rec_inputs():
        import jax
        import jax.numpy as jnp
        _rk = jax.random.key(seed)
        x = -0.0003929 + 0.9999 * jax.random.normal(jax.random.fold_in(_rk, 1), (8, 256, 256), jnp.float32)
        _lenS = 256 - jax.random.randint(jax.random.fold_in(_rk, 7), (8,), 0, max(1, 256 // 4) + 1, jnp.int32)
        _lenS2 = 77 - jax.random.randint(jax.random.fold_in(_rk, 8), (8,), 0, max(1, 77 // 4) + 1, jnp.int32)
        _ctx_768P = jax.random.normal(jax.random.fold_in(_rk, 11), (8, 16, 192), jnp.float32)
        _ctx_768c = jax.random.dirichlet(jax.random.fold_in(_rk, 511), 0.3 * jnp.ones((16,), jnp.float32), (8, 77))
        _ctx_768t = jnp.einsum('bsk,bkd->bsd', _ctx_768c, _ctx_768P)
        _ctx_768t = _ctx_768t * jax.lax.rsqrt(jnp.mean(jnp.square(_ctx_768t)) + 1e-12) * 0.953939
        ctx_768 = -7.36909e-05 + 0.999899 * (_ctx_768t + 0.3 * jax.random.normal(jax.random.fold_in(_rk, 611), (8, 77, 192), jnp.float32))
        return (x, ctx_768)
    x, ctx_768 = _rec_inputs()

    def _L0_attn_setup():
        import jax, jax.numpy as jnp
        import numpy as np
        import math
        D_MODEL = 256
        N_HEADS = 16
        D_HEAD = D_MODEL // N_HEADS
        WINDOW = 64
        SCALE = 1.0 / math.sqrt(D_HEAD)

        def _window_mask(seq_len: int) -> jnp.ndarray:
            i = jnp.arange(seq_len)[:, None]
            j = jnp.arange(seq_len)[None, :]
            allowed = (j <= i) & (j > i - WINDOW)
            return jnp.where(allowed, 0.0, -jnp.inf).astype(jnp.float32)
        key = jax.random.key(seed)
        kx, kqkv, kout = jax.random.split(key, 3)
        x = jax.random.normal(kx, (2, 512, D_MODEL), dtype=jnp.float32)
        lim_qkv = math.sqrt(6.0 / (D_MODEL + 3 * D_MODEL))
        W_qkv = jax.random.uniform(kqkv, (D_MODEL, 3 * D_MODEL), dtype=jnp.float32, minval=-lim_qkv, maxval=lim_qkv)
        lim_out = math.sqrt(6.0 / (D_MODEL + D_MODEL))
        W_out = jax.random.uniform(kout, (D_MODEL, D_MODEL), dtype=jnp.float32, minval=-lim_out, maxval=lim_out)
        return {'x': x, 'W_qkv': W_qkv, 'W_out': W_out}
    _L0_attn_all = _L0_attn_setup()
    _L0_attn_in = {k: v for k, v in _L0_attn_all.items() if k in ('W_qkv', 'W_out')}
    del _L0_attn_all

    def _L0_xattn_setup():
        import jax, jax.numpy as jnp
        import numpy as np
        IMG_DIM, TXT_DIM, HID = (256, 192, 256)
        B, LQ, LK = (8, 512, 512)
        key = jax.random.key(seed)
        ks = jax.random.split(key, 8)
        s_img = 1.0 / np.sqrt(IMG_DIM)
        s_txt = 1.0 / np.sqrt(TXT_DIM)
        return {'image_features': jax.random.normal(ks[0], (B, LQ, IMG_DIM), jnp.float32), 'text_features': jax.random.normal(ks[1], (B, LK, TXT_DIM), jnp.float32), 'Wq': jax.random.uniform(ks[2], (IMG_DIM, HID), jnp.float32, -s_img, s_img), 'bq': jax.random.uniform(ks[3], (HID,), jnp.float32, -s_img, s_img), 'Wk': jax.random.uniform(ks[4], (TXT_DIM, HID), jnp.float32, -s_txt, s_txt), 'bk': jax.random.uniform(ks[5], (HID,), jnp.float32, -s_txt, s_txt), 'Wv': jax.random.uniform(ks[6], (TXT_DIM, HID), jnp.float32, -s_txt, s_txt), 'bv': jax.random.uniform(ks[7], (HID,), jnp.float32, -s_txt, s_txt)}
    _L0_xattn_all = _L0_xattn_setup()
    _L0_xattn_in = {k: v for k, v in _L0_xattn_all.items() if k in ('Wq', 'bq', 'Wk', 'bk', 'Wv', 'bv')}
    del _L0_xattn_all

    def _L0_ffn_setup():
        import jax, jax.numpy as jnp
        import numpy as np
        DMODEL = 256
        N_EXPERTS = 32
        EXPERT_SIZE = 128
        N_HEADS = 4
        WEIGHT_SCALE = 1.0
        key = jax.random.key(seed)
        k0, k1, k2, k3 = jax.random.split(key, 4)
        x = jax.random.normal(k0, (2, 512, DMODEL), dtype=jnp.float32)
        expert_sel = jax.random.normal(k1, (N_EXPERTS, DMODEL), dtype=jnp.float32) * DMODEL ** (-0.5)
        keys = jax.random.normal(k2, (N_EXPERTS, DMODEL, EXPERT_SIZE), dtype=jnp.float32) * DMODEL ** (-0.5)
        values = jax.random.normal(k3, (N_EXPERTS, EXPERT_SIZE, DMODEL), dtype=jnp.float32) * (N_EXPERTS * EXPERT_SIZE) ** (-0.5)
        return {'x': x, 'expert_sel': expert_sel, 'keys': keys, 'values': values}
    _L0_ffn_all = _L0_ffn_setup()
    _L0_ffn_in = {k: v for k, v in _L0_ffn_all.items() if k in ('expert_sel', 'keys', 'values')}
    del _L0_ffn_all
    return {'x': x, 'ctx_768': ctx_768, 'L0_attn_W_qkv': _L0_attn_in['W_qkv'], 'L0_attn_W_out': _L0_attn_in['W_out'], 'L0_xattn_Wq': _L0_xattn_in['Wq'], 'L0_xattn_bq': _L0_xattn_in['bq'], 'L0_xattn_Wk': _L0_xattn_in['Wk'], 'L0_xattn_bk': _L0_xattn_in['bk'], 'L0_xattn_Wv': _L0_xattn_in['Wv'], 'L0_xattn_bv': _L0_xattn_in['bv'], 'L0_ffn_expert_sel': _L0_ffn_in['expert_sel'], 'L0_ffn_keys': _L0_ffn_in['keys'], 'L0_ffn_values': _L0_ffn_in['values']}

def reference(x, ctx_768, L0_attn_W_qkv, L0_attn_W_out, L0_xattn_Wq, L0_xattn_bq, L0_xattn_Wk, L0_xattn_bk, L0_xattn_Wv, L0_xattn_bv, L0_ffn_expert_sel, L0_ffn_keys, L0_ffn_values):
    import jax
    import jax.numpy as jnp

    def _L0_attn_ref(x, W_qkv, W_out):
        import jax, jax.numpy as jnp
        import numpy as np
        import math
        D_MODEL = 256
        N_HEADS = 16
        D_HEAD = D_MODEL // N_HEADS
        WINDOW = 64
        SCALE = 1.0 / math.sqrt(D_HEAD)

        def _window_mask(seq_len: int) -> jnp.ndarray:
            i = jnp.arange(seq_len)[:, None]
            j = jnp.arange(seq_len)[None, :]
            allowed = (j <= i) & (j > i - WINDOW)
            return jnp.where(allowed, 0.0, -jnp.inf).astype(jnp.float32)
        B, S, _ = x.shape
        qkv = x @ W_qkv
        qkv = qkv.reshape(B, S, 3, N_HEADS, D_HEAD)
        qkv = jnp.transpose(qkv, (2, 0, 3, 1, 4))
        q, k, v = (qkv[0], qkv[1], qkv[2])
        scores = jnp.einsum('bhsd,bhtd->bhst', q, k) * SCALE
        scores = scores + _window_mask(S)[None, None]
        weights = jax.nn.softmax(scores, axis=-1)
        out = jnp.einsum('bhst,bhtd->bhsd', weights, v)
        out = jnp.transpose(out, (0, 2, 1, 3)).reshape(B, S, D_MODEL)
        return out @ W_out

    def _L0_xattn_ref(image_features, text_features, Wq, bq, Wk, bk, Wv, bv):
        import jax, jax.numpy as jnp
        import numpy as np
        IMG_DIM, TXT_DIM, HID = (256, 192, 256)
        B, LQ, LK = (8, 512, 512)
        query = jnp.einsum('bqi,ih->bqh', image_features, Wq) + bq
        key = jnp.einsum('bkt,th->bkh', text_features, Wk) + bk
        value = jnp.einsum('bkt,th->bkh', text_features, Wv) + bv
        scale = 1.0 / jnp.sqrt(jnp.asarray(HID, query.dtype))
        scores = jnp.einsum('bqh,bkh->bqk', query, key) * scale
        weights = jax.nn.softmax(scores, axis=-1)
        attended = jnp.einsum('bqk,bkh->bqh', weights, value)
        return attended

    def _L0_ffn_ref(x, expert_sel, keys, values):
        import jax, jax.numpy as jnp
        import numpy as np
        DMODEL = 256
        N_EXPERTS = 32
        EXPERT_SIZE = 128
        N_HEADS = 4
        WEIGHT_SCALE = 1.0
        B, S, D = x.shape
        xt = x.reshape(-1, D)
        N = xt.shape[0]
        sel_logits = jnp.einsum('nd,ed->ne', xt, expert_sel)
        gates = jax.nn.sigmoid(sel_logits)
        sel_val, sel_idx = jax.lax.top_k(gates, N_HEADS)
        gate_full = jnp.zeros_like(gates).at[jnp.arange(N)[:, None], sel_idx].set(sel_val)
        scores = jax.nn.relu(jnp.einsum('nd,edf->nef', xt, keys))
        scores = scores * gate_full[:, :, None]
        out = jnp.einsum('nef,efv->nv', scores, values)
        return out.reshape(B, S, -1)
    x = _layernorm(x + _L0_attn_ref(x, L0_attn_W_qkv, L0_attn_W_out), axis=-1)
    x = _layernorm(x + _L0_xattn_ref(x, ctx_768, L0_xattn_Wq, L0_xattn_bq, L0_xattn_Wk, L0_xattn_bk, L0_xattn_Wv, L0_xattn_bv), axis=-1)
    x = _layernorm(x + _L0_ffn_ref(x, L0_ffn_expert_sel, L0_ffn_keys, L0_ffn_values), axis=-1)
    return x

_drawn_inputs = setup_inputs


def setup_inputs(seed=0):
    import zlib

    import numpy as np

    out = dict(_drawn_inputs(seed))
    spreads = {}
    factors = {'L0_xattn_bq': 5.093, 'L0_xattn_bk': 8.0}
    for name, (base, spread) in spreads.items():
        noise = np.random.default_rng([zlib.crc32(name.encode()), seed]).standard_normal(out[name].shape)
        drawn = base * np.exp(spread * noise) if base else spread * noise
        out[name] = jnp.asarray(drawn.astype(out[name].dtype))
    for name, factor in factors.items():
        out[name] = (out[name] * factor).astype(out[name].dtype)
    return out
```

```python
from contextlib import ExitStack

import concourse.bass as bass
from concourse import mybir

F32 = mybir.dt.float32
BF16 = mybir.dt.bfloat16
I32 = mybir.dt.int32
U32 = mybir.dt.uint32
ALU = mybir.AluOpType
ACT = mybir.ActivationFunctionType
AX = mybir.AxisListType

P = 128
NEG = -1.0e30
MAGIC = 12582912.0
LN_EPS = 1e-5


def decoder_layer(nc, x, ctx_in, w_qkv, w_out, wq, bq, wk, bk, wv, bv, expert_sel, keys, values, out, rows_dram, parts_dram):
    B, S, D = x.shape
    LK, TXT = ctx_in.shape[1:]
    NE, _, ES = keys.shape
    TOPK, HEADS, DH, WIN = 4, 16, 16, 64
    DC = D // P
    TB = S // P
    NT = B * TB
    PAIRS = HEADS // 2
    HC = HEADS // DC
    GP = PAIRS // DC
    NQ = S // WIN
    NG = NQ * DC
    VC = 2 * DH + 1
    TXT2 = TXT - P
    ROW = D + 2
    SEG = B * S + P
    FULL = B * S * TOPK // P
    TABLE_STEPS = 15
    PAD_ID = 1 << 20

    with ExitStack() as stack:
        def sb(name, shape, dt=F32):
            return stack.enter_context(nc.sbuf_tensor(name, shape, dt))

        def ps(name):
            return stack.enter_context(nc.psum_tensor(name, [P, 512], F32))

        def sem(name):
            return stack.enter_context(nc.semaphore(name))

        ident = sb("ident", [P, P])
        ident_bf = sb("ident_bf", [P, P], BF16)
        mask = sb("mask", [P, GP, P], BF16)
        mask0 = sb("mask0", [P, GP, WIN], BF16)
        earlier = sb("earlier", [P, P], BF16)
        ones_bf = sb("ones_bf", [P, P], BF16)
        zeros = sb("zeros", [P, NE])
        e_index = sb("e_index", [P, TB * TOPK, NE])
        e_start = sb("e_start", [P, TB, NE])
        row_id = sb("row_id", [P, TB, TOPK], I32)
        eps_col = sb("eps_col", [P, 1])
        pad_rows = sb("pad_rows", [P, ROW])
        part_no = sb("part_no", [P, 1])
        wqkv_sb = sb("wqkv_sb", [P, DC, 3 * D])
        wo_sb = sb("wo_sb", [P, 2, D])
        wq_sb = sb("wq_sb", [P, DC, D])
        wk_sb = sb("wk_sb", [P, D])
        wk2_sb = sb("wk2_sb", [TXT2, D])
        wv_sb = sb("wv_sb", [P, D])
        wv2_sb = sb("wv2_sb", [TXT2, D])
        bq_sb = sb("bq_sb", [P, DC])
        bk_sb = sb("bk_sb", [P, DC])
        bv_sb = sb("bv_sb", [LK, D])
        sel_rows = sb("sel_rows", [NE, D])
        sel_t = sb("sel_t", [P, DC, NE])
        keys_sb = sb("keys_sb", [P, NE, DC, ES])
        values_sb = sb("values_sb", [P, NE, D])
        ctx_sb = sb("ctx_sb", [LK, B, TXT])
        ctx_t = sb("ctx_t", [P, B * LK])
        ctx2_t = sb("ctx2_t", [TXT2, B * LK])
        k2t = sb("k2t", [P, DC, B * LK])
        v2 = sb("v2", [LK, B, D])
        xf = sb("xf", [P, TB, D])
        xr = sb("xr", [P, TB, D])
        xt = sb("xt", [P, DC, S])
        qt = sb("qt", [P, DC, S])
        qx = sb("qx", [P, DC * NQ, HC, WIN])
        kt = sb("kt", [P, DC, S])
        vw = sb("vw", [P, 3, PAIRS, VC])
        pb = [sb(f"pb{i}", [P, GP * P]) for i in range(2)]
        pt = [sb(f"pt{i}", [P, GP * P]) for i in range(2)]
        mx = [sb(f"mx{i}", [P, GP]) for i in range(2)]
        rs = [sb(f"rs{i}", [P, GP]) for i in range(2)]
        att = sb("att", [P, NQ, P])
        att_t = sb("att_t", [P, 2, S])
        r1 = sb("r1", [P, TB, D])
        x1 = sb("x1", [P, TB, D])
        x1t = sb("x1t", [P, DC, S])
        st1 = sb("st1", [P, TB, 6])
        mv1 = sb("mv1", [P, TB, 2])
        lnv = sb("lnv", [P, 6, TB])
        st2 = sb("st2", [P, TB, 6])
        mv2 = sb("mv2", [P, TB, 2])
        lnv2 = sb("lnv2", [P, 6, TB])
        q2t = sb("q2t", [P, DC, S])
        cmx = sb("cmx", [P, TB])
        cneg = sb("cneg", [P, TB])
        csum = sb("csum", [P, TB])
        crec = sb("crec", [P, TB])
        p2 = sb("p2", [P, TB, LK])
        p2t = sb("p2t", [LK, TB, P])
        r2 = sb("r2", [P, TB, D])
        xs = sb("xs", [P, TB, TOPK, ROW])
        x2t = sb("x2t", [P, DC, S])
        ex = sb("ex", [P, TB, NE])
        ex1 = sb("ex1", [P, TB, NE])
        gates = sb("gates", [P, TB, NE])
        top_v = sb("top_v", [P, TB, 8])
        top_i = sb("top_i", [P, TB, 8], U32)
        top_f = sb("top_f", [P, TB, TOPK])
        onehot = sb("onehot", [P, TB * TOPK, NE])
        picked = sb("picked", [P, TB, NE], BF16)
        so_far = sb("so_far", [P, NE], BF16)
        place = sb("place", [P, TB, NE])
        prod = sb("prod", [P, TB * TOPK, NE])
        slot_f = sb("slot_f", [P, TB * TOPK])
        slot = sb("slot", [P, TB * TOPK], U32)
        x2_all = sb("x2_all", [P, NT, D])

        bank_s = [ps(f"bank_s{i}") for i in range(2)]
        bank_t = [ps(f"bank_t{i}") for i in range(2)]
        bank_o = ps("bank_o")
        bank_m = [ps(f"bank_m{i}") for i in range(3)]

        JOBS = ["xt", "x2t", "q", "lg", "k", "v", "at", "op", "rk", "x1t", "cq", "cs", "p2t", "co"]
        LATE = {**{j: 0 for j in ("xt", "q", "k", "v")},
                **{j: 1 for j in ("at", "op", "x1t", "cq", "cs", "p2t", "co")},
                **{j: 2 for j in ("x2t", "lg", "rk")}}
        job_bank = {j: bank_m[n % 3] for n, j in enumerate(JOBS)}
        done = {j: sem("pe_" + j) for j in JOBS}
        freed = {j: sem("free_" + j) for j in JOBS}

        weights_in = sem("weights_in")
        experts_in = sem("experts_in")
        consts = sem("consts")
        chain_p = sem("chain_p")
        ln1_step = sem("ln1_step")
        ln2_step = sem("ln2_step")
        topk_step = sem("topk_step")
        slot_step = sem("slot_step")
        ln3_step = sem("ln3_step")
        stats_done = sem("stats_done")
        row_id_done = sem("row_id_done")
        cmx_done = sem("cmx_done")
        ln_done = [sem("ln1_log"), sem("ln2_log")]
        pro_pe = sem("pro_pe")
        pro_ev = sem("pro_ev")
        xf_in = sem("xf_in")
        xr_in = sem("xr_in")
        qx_in = [sem(f"qx_in{i}") for i in range(GP)]
        vw_in = sem("vw_in")
        s_ready = sem("s_ready")
        mx_done = sem("mx_done")
        sub_done = sem("sub_done")
        exp_done = sem("exp_done")
        t_done = sem("t_done")
        pt_done = sem("pt_done")
        pv_done = sem("pv_done")
        rs_done = sem("rs_done")
        norm_done = sem("norm_done")
        var_done = [sem("var1_done"), sem("var2_done")]
        rstd_done = [sem("rstd1_done"), sem("rstd2_done")]
        x1_done = sem("x1_done")
        x2_done = sem("x2_done")
        x2_kept = sem("x2_kept")
        cneg_done = sem("cneg_done")
        p2_done = sem("p2_done")
        picked_done = sem("picked_done")
        slots_done = sem("slots_done")
        scattered = sem("scattered")
        pads_in = sem("pads_in")
        out_in = sem("out_in")

        xg = [sb(f"xg{i}", [P, 2, ROW]) for i in range(2)]
        ids = [sb(f"ids{i}", [P, 2], I32) for i in range(4)]
        gate_col = [sb(f"gate_col{i}", [P, 2]) for i in range(2)]
        xgt = [sb(f"xgt{i}", [P, 2, DC, P]) for i in range(2)]
        hr = [sb(f"hr{i}", [P, 2, ES]) for i in range(2)]
        ht = [sb(f"ht{i}", [P, 2, P]) for i in range(2)]
        spare = qx[:].rearrange("p n h q -> p (n h q)")
        yb = [spare[:, i * 2 * D:(i + 1) * 2 * D].rearrange("p (j d) -> p j d", j=2) for i in range(2)]
        counts = sb("counts", [P, NE])
        fulls = sb("fulls", [P, NE])
        full_end = sb("full_end", [P, NE])
        ended = sb("ended", [P, NE])
        ended_n = sb("ended_n", [P, NE])
        tile_col = sb("tile_col", [P, 8])
        row_tab = sb("row_tab", [1, FULL + NE], I32)
        exp_tab = sb("exp_tab", [1, FULL + NE], I32)
        pad_tab = sb("pad_tab", [1, NE], I32)
        counted = sem("counted")
        turned = sem("turned")
        tables = sem("tables")
        table_step = sem("table_step")
        xg_in = [sem(f"xg_in{i}") for i in range(2)]
        ids_kept = sem("ids_kept")
        gate_kept = sem("gate_kept")
        gx_done = sem("gx_done")
        gx_copied = sem("gx_copied")
        h_done = sem("h_done")
        h_gated = sem("h_gated")
        ht_done = sem("ht_done")
        ht_copied = sem("ht_copied")
        y_done = sem("y_done")
        y_copied = sem("y_copied")
        y_sent = [sem(f"y_sent{i}") for i in range(2)]
        parts_sb = [spare[:, (4 + i * TOPK) * D:(8 + i * TOPK) * D].rearrange("p (k d) -> p k d", k=TOPK) for i in range(2)]
        half = [spare[:, (12 + 2 * i) * D:(14 + 2 * i) * D].rearrange("p (k d) -> p k d", k=2) for i in range(2)]
        quarter = sb("quarter", [P, D])
        st3 = sb("st3", [P, NT, 6])
        ln3 = sb("ln3", [P, 8, NT])
        parts_in = [sem(f"parts_in{i}") for i in range(2)]
        half_done = sem("half_done")
        sum_step = sem("sum_step")
        var3_done = sem("var3_done")
        rstd3_done = sem("rstd3_done")
        out_ready = sem("out_ready")

        NTILES = FULL + NE
        NP2 = NTILES // 2

        passed = {}

        def w(eng, s, n):
            if not isinstance(n, int) or n > 0:
                eng.wait_ge(s, n)
            if not isinstance(n, int):
                eng.sem_inc(passed[eng_name(eng)], 1)

        def eng_name(eng):
            return str(eng.engine)

        def bank_free(eng, job, b):
            n = JOBS.index(job)
            last = JOBS[n - 3] if n >= 3 else JOBS[{0: 12, 1: 13, 2: 11}[n]]
            count = b - LATE[last] + (1 if n >= 3 else 0)
            w(eng, freed[last], min(count, B) if isinstance(b, int) else count)

        class Steps:
            def __init__(self, eng, s, per):
                self.eng, self.sem, self.per = eng, s, per

            def begin(self, b):
                self.base, self.n = b * self.per, 0

            def link(self, ins):
                self.n += 1
                ins.then_inc(self.sem, 1)
                self.eng.wait_ge(self.sem, self.base + self.n)

            def end(self):
                assert self.n == self.per, (self.n, self.per)

        def keys_of(qb):
            return (0, WIN) if qb == 0 else (WIN * (qb - 1), P)

        for e in (nc.tensor, nc.vector, nc.scalar, nc.gpsimd, nc.sync):
            passed[eng_name(e)] = sem("passed_" + eng_name(e).split(".")[-1])

        block = stack.enter_context(nc.Block())

        @block.sync
        def _(sp):
            def x_of(b):
                return x[bass.ds(b, 1)].rearrange("a (t p) d -> p (a t) d", p=P)

            sp.dma_start(xf[:], x_of(0)).then_inc(xf_in, 16)
            sp.dma_start(wqkv_sb[:], w_qkv.rearrange("(c p) n -> p c n", p=P)).then_inc(weights_in, 16)
            sp.dma_start(ctx_sb[:], ctx_in.rearrange("b k t -> k b t")).then_inc(weights_in, 16)
            sp.dma_start(wk_sb[:], wk[0:P, :]).then_inc(weights_in, 16)
            sp.dma_start(wk2_sb[:], wk[P:TXT, :]).then_inc(weights_in, 16)
            sp.dma_start(wv_sb[:], wv[0:P, :]).then_inc(weights_in, 16)
            sp.dma_start(wv2_sb[:], wv[P:TXT, :]).then_inc(weights_in, 16)
            sp.dma_start(bk_sb[:], bk.rearrange("(c p) -> p c", p=P), allow_slow_non_contiguous=True).then_inc(weights_in, 16)
            sp.dma_start(bq_sb[:], bq.rearrange("(c p) -> p c", p=P), allow_slow_non_contiguous=True).then_inc(weights_in, 16)
            sp.dma_start(bv_sb[:], bv.partition_broadcast(LK)).then_inc(weights_in, 16)
            sp.dma_start(sel_rows[:], expert_sel).then_inc(weights_in, 16)
            sp.dma_start(wq_sb[:], wq.rearrange("(c p) n -> p c n", p=P)).then_inc(weights_in, 16)
            w_heads = w_out.rearrange("(a r d) n -> a d r n", r=2, d=DH)
            for a in range(PAIRS):
                sp.dma_start(wo_sb[DH * a:DH * a + DH], w_heads[a]).then_inc(weights_in, 16)
            sp.dma_start(xr[:], x_of(0)).then_inc(xr_in, 16)

            def spread(b):
                w(sp, freed["q"], b + 1)
                w(sp, s_ready, NG * b)
                for j in range(HC):
                    sp.dma_start(qx[DH * j:DH * j + DH, :, j, :],
                                 qt[DH * j:DH * j + DH, :, :].rearrange("p c (n q) -> p (c n) q", q=WIN)).then_inc(qx_in[j // 2], 16)
                w(sp, freed["v"], b + 1)
                sp.dma_start(vw[0:WIN, 2], vw[WIN:P, 0]).then_inc(vw_in, 16)
                sp.dma_start(vw[WIN:P, 2], vw[0:WIN, 1]).then_inc(vw_in, 16)

            def next_x(b):
                w(sp, done["xt"], b)
                sp.dma_start(xf[:], x_of(b)).then_inc(xf_in, 16)

            def next_residual(b):
                w(sp, freed["op"], b)
                sp.dma_start(xr[:], x_of(b)).then_inc(xr_in, 16)

            def keep_x2(b):
                w(sp, x2_done, TB * (b + 1))
                sp.dma_start(x2_all[:, bass.ds(b * TB, TB), :], xs[:, :, 0, 0:D]).then_inc(x2_kept, 16)

            next_x(1)
            spread(0)
            n = NE // 4
            for i in range(4):
                for c in range(DC):
                    sp.dma_start(keys_sb[:, n * i:n * i + n, c, :],
                                 keys[n * i:n * i + n, c * P:c * P + P, :].rearrange("e p f -> p e f")).then_inc(experts_in, 16)
                sp.dma_start(values_sb[:, n * i:n * i + n, :],
                             values[n * i:n * i + n].rearrange("e f v -> f e v")).then_inc(experts_in, 16)
            sp.dma_start(rows_dram[NE * SEG:NE * SEG + P, :], pad_rows[:]).then_inc(pads_in, 16)
            with sp.Fori(1, B - 1) as b:
                next_x(b + 1)
                spread(b)
                next_residual(b)
                keep_x2(b - 1)
            spread(B - 1)
            next_residual(B - 1)
            keep_x2(B - 2)
            keep_x2(B - 1)

            w(sp, tables, 1)
            with sp.Fori(0, NE) as e:
                r = sp.value_load(pad_tab[0:1, bass.ds(e, 1)], min_val=0, max_val=NE * SEG - P)
                sp.dma_start(rows_dram[bass.ds(r, P), :], pad_rows[:]).then_inc(pads_in, 16)
            w(sp, pads_in, 16 * (NE + 1))
            w(sp, tables, 4)
            w(sp, scattered, 16 * TB * TOPK * B)

            def rows_of(i, par):
                w(sp, gx_done, i - 1)
                w(sp, gate_kept, i - 1)
                w(sp, ids_kept, i - 1)
                for j in range(2):
                    r = sp.value_load(row_tab[0:1, bass.ds(i * 2 + j, 1)], min_val=0, max_val=NE * SEG)
                    sp.dma_start(xg[par][:, j, :], rows_dram[bass.ds(r, P), :]).then_inc(xg_in[par], 16)

            rows_of(0, 0)
            rows_of(1, 1)
            with sp.Fori(1, NP2 // 2) as m:
                rows_of(m * 2, 0)
                rows_of(m * 2 + 1, 1)

            for par in range(2):
                w(sp, y_sent[par], 32 * (NP2 // 2))
            parts = parts_dram.rearrange("(t p k) d -> t p k d", p=P, k=TOPK)

            def parts_of(t, par):
                w(sp, half_done, t - 1)
                sp.dma_start(parts_sb[par], parts[bass.ds(t, 1)].rearrange("a p k d -> (a p) k d")).then_inc(parts_in[par], 16)

            parts_of(0, 0)
            parts_of(1, 1)
            with sp.Fori(1, NT // 2) as m:
                parts_of(m * 2, 0)
                parts_of(m * 2 + 1, 1)
            out_tiles = out.rearrange("b (t p) d -> p (b t) d", p=P)
            for q in range(4):
                n = NT // 4
                w(sp, out_ready, n * (q + 1))
                sp.dma_start(out_tiles[:, n * q:n * q + n, :], x2_all[:, n * q:n * q + n, :]).then_inc(out_in, 16)
            w(sp, out_in, 64)

        @block.gpsimd
        def _(pool):
            count = [0]

            def link(ins):
                count[0] += 1
                ins.then_inc(chain_p, 1)
                w(pool, chain_p, count[0])

            link(pool.memset(ident[:], 0.0))
            link(pool.affine_select(out=ident[:], in_=ident[:], compare_op=ALU.not_equal, fill=1.0, base=0,
                                    pattern=[[-1, P]], channel_multiplier=1))
            link(pool.memset(ident_bf[:], 0.0))
            link(pool.affine_select(out=ident_bf[:], in_=ident_bf[:], compare_op=ALU.not_equal, fill=1.0, base=0,
                                    pattern=[[-1, P]], channel_multiplier=1))
            link(pool.memset(qx[:], 0.0))
            link(pool.memset(vw[:, :, :, 2 * DH:VC], 1.0))
            link(pool.memset(mask[:], 0.0))
            link(pool.memset(mask0[:], 0.0))
            for h in range(2):
                q = slice(WIN * h, WIN * h + WIN)
                link(pool.affine_select(out=mask[q], in_=mask[q], compare_op=ALU.is_gt, fill=NEG, base=0,
                                        pattern=[[0, GP], [1, P]], channel_multiplier=-1))
                link(pool.affine_select(out=mask[q], in_=mask[q], compare_op=ALU.is_ge, fill=NEG, base=WIN,
                                        pattern=[[0, GP], [-1, P]], channel_multiplier=1))
                link(pool.affine_select(out=mask0[q], in_=mask0[q], compare_op=ALU.is_ge, fill=NEG, base=0,
                                        pattern=[[0, GP], [-1, WIN]], channel_multiplier=1))
            link(pool.memset(ones_bf[:], 1.0))
            link(pool.memset(earlier[:], 1.0))
            link(pool.affine_select(out=earlier[:], in_=earlier[:], compare_op=ALU.is_gt, fill=0.0, base=0,
                                    pattern=[[1, P]], channel_multiplier=-1))
            link(pool.memset(zeros[:], 0.0))
            link(pool.memset(so_far[:], 0.0))
            link(pool.memset(eps_col[:], LN_EPS))
            link(pool.iota(e_index[:], pattern=[[0, TB * TOPK], [1, NE]], base=0, channel_multiplier=0,
                           allow_small_or_imprecise_dtypes=True))
            link(pool.iota(e_start[:], pattern=[[0, TB], [SEG, NE]], base=0, channel_multiplier=0,
                           allow_small_or_imprecise_dtypes=True))
            link(pool.iota(row_id[:], pattern=[[P * TOPK, TB], [1, TOPK]], base=0, channel_multiplier=TOPK))
            link(pool.iota(part_no[:], pattern=[[0, 1]], base=0, channel_multiplier=1,
                           allow_small_or_imprecise_dtypes=True))
            link(pool.iota(exp_tab[:, FULL:NTILES], pattern=[[1, NE]], base=0, channel_multiplier=0))
            link(pool.memset(pad_rows[:], 0.0))
            pool.iota(pad_rows[:, D:D + 1].bitcast(I32), pattern=[[0, 1]], base=PAD_ID, channel_multiplier=0)\
                .then_inc(consts, 1)

            def scatter(b):
                w(pool, slots_done, b + 1)
                for t in range(TB):
                    for k in range(TOPK):
                        n = t * TOPK + k
                        pool.indirect_dma_start(rows_dram, bass.IndirectOffsetOnAxis(ap=slot[:, n:n + 1], axis=0),
                                                xs[:, t, k, :], None).then_inc(scattered, 16)

            with pool.Fori(0, B) as b:
                scatter(b)

            def send(i, k):
                w(pool, y_copied, i + 1)
                for j in range(2):
                    pool.indirect_dma_start(parts_dram, bass.IndirectOffsetOnAxis(ap=ids[k][:, j:j + 1].bitcast(U32), axis=0),
                                            yb[k % 2][:, j, :], None, bounds_check=B * S * TOPK - 1,
                                            oob_is_err=False).then_inc(y_sent[k % 2], 16)

            with pool.Fori(0, NP2 // 4) as m:
                for k in range(4):
                    send(m * 4 + k, k)

            def halves(t, par, m):
                w(pool, parts_in[par], m * 16 + 16)
                w(pool, sum_step, (t - 1) * 2)
                pool.tensor_tensor(out=half[par], in0=parts_sb[par][:, 0:2, :], in1=parts_sb[par][:, 2:4, :],
                                   op=ALU.add).then_inc(half_done, 1)

            halves(0, 0, 0)
            halves(1, 1, 0)
            with pool.Fori(1, NT // 2) as m:
                halves(m * 2, 0, m)
                halves(m * 2 + 1, 1, m)

        @block.tensor
        def _(pe):
            pe.wait_ge(consts, 1)
            pe.wait_ge(weights_in, 16 * (11 + PAIRS))
            HB = B // 2
            for h in range(2):
                for i in range(HB):
                    n = h * HB + i
                    pe.transpose(bank_s[h][:, i * LK:i * LK + LK], ctx_sb[:, n, 0:P], ident[0:LK, 0:LK])
                    last = pe.transpose(bank_t[h][0:TXT2, i * LK:i * LK + LK], ctx_sb[:, n, P:TXT], ident[0:LK, 0:LK])
            for c in range(DC):
                last = pe.transpose(bank_o[:, c * NE:c * NE + NE], sel_rows[:, c * P:c * P + P], ident[0:NE, 0:NE])
            last.then_inc(pro_pe, 1)
            pe.wait_ge(pro_ev, 5)
            for n in range(B):
                bank = [*bank_m, bank_o][n // 2]
                o = bank[0:LK, n % 2 * D:n % 2 * D + D]
                pe.matmul(o, ctx_t[:, n * LK:n * LK + LK], wv_sb[:], start=True, stop=False)
                last = pe.matmul(o, ctx2_t[:, n * LK:n * LK + LK], wv2_sb[:], start=False, stop=True)
            last.then_inc(pro_pe, 1)
            for c in range(DC):
                for h in range(2):
                    bank = [*bank_s, *bank_t][2 * c + h]
                    o = bank[:, 0:HB * LK]
                    f = slice(h * HB * LK, (h + 1) * HB * LK)
                    pe.matmul(o, wk_sb[:, c * P:c * P + P], ctx_t[:, f], start=True, stop=False)
                    last = pe.matmul(o, wk2_sb[:, c * P:c * P + P], ctx2_t[:, f], start=False, stop=True)
            last.then_inc(pro_pe, 1)
            pe.wait_ge(pro_ev, 13)

            def turn(job, b, src):
                bank_free(pe, job, b)
                for c in range(DC):
                    for t in range(TB):
                        o = job_bank[job][:, c * S + t * P:c * S + t * P + P]
                        last = pe.transpose(o, src(t, c), ident[:])
                last.then_inc(done[job], 1)

            def project(job, b, weights, src):
                bank_free(pe, job, b)
                for c in range(DC):
                    for k in range(DC):
                        last = pe.matmul(job_bank[job][:, c * S:c * S + S], weights(k, c), src[:, k, :],
                                         start=(k == 0), stop=(k == DC - 1))
                last.then_inc(done[job], 1)

            def project_rows(job, b, src, weights):
                bank_free(pe, job, b)
                for t in range(TB):
                    for k in range(DC):
                        last = pe.matmul(job_bank[job][:, t * D:t * D + D], src[:, k, t * P:t * P + P], weights(k),
                                         start=(k == 0), stop=(k == DC - 1))
                last.then_inc(done[job], 1)

            def score(b, g):
                qb, c = g // DC, g % DC
                k0, kw = keys_of(qb)
                n = b * NG + g
                o = bank_s[g % 2]
                w(pe, sub_done, n - 1)
                pe.matmul(o[:, 0:GP * kw], ident_bf[:], (mask0 if qb == 0 else mask)[:].rearrange("p a j -> p (a j)"),
                          start=True, stop=False, skip_group_check=True)
                for a in range(GP):
                    if g == 0:
                        pe.wait_ge(qx_in[a], b * 32 + 32)
                    last = pe.matmul(o[:, a * kw:a * kw + kw], qx[:, c * NQ + qb, 2 * a:2 * a + 2, :].rearrange("p h q -> p (h q)"),
                                     kt[:, c, k0:k0 + kw], start=False, stop=True, skip_group_check=True)
                last.then_inc(s_ready, 1)

            def turn_probs(b, g):
                kw = keys_of(g // DC)[1]
                n = b * NG + g
                pe.wait_ge(exp_done, n + 1)
                w(pe, pt_done, n - 1)
                for a in range(GP):
                    last = pe.transpose(bank_t[g % 2][0:kw, a * P:a * P + P], pb[g % 2][:, a * kw:a * kw + kw], ident[:])
                last.then_inc(t_done, 1)

            def attend(b, g):
                qb, c = g // DC, g % DC
                kw = keys_of(qb)[1]
                n = b * NG + g
                window = [0, 0, 2, 1][qb]
                pe.wait_ge(pt_done, n + 1)
                w(pe, norm_done, 2 * n)
                if g == 0:
                    pe.wait_ge(freed["v"], b + 1)
                if g == 2 * DC:
                    pe.wait_ge(vw_in, b * 32 + 32)
                for a in range(GP):
                    last = pe.matmul(bank_o[:, a * VC:a * VC + VC], pt[g % 2][0:kw, a * P:a * P + P],
                                     vw[0:kw, window, c * GP + a, :], start=True, stop=True)
                last.then_inc(pv_done, 1)

            def round_(b, front, tail, late):
                t1, t2 = b - 1, b - 2
                if tail:
                    turn_probs(t1, NG - 1)
                if front:
                    pe.wait_ge(xf_in, b * 16 + 16)
                    turn("xt", b, lambda t, c: xf[:, t, c * P:c * P + P])
                if late:
                    pe.wait_ge(x2_done, t2 * TB + TB)
                    turn("x2t", b, lambda t, c: xs[:, t, 0, c * P:c * P + P])
                if tail:
                    attend(t1, NG - 2)
                if front:
                    pe.wait_ge(freed["xt"], b + 1)
                    project("q", b, lambda k, c: wqkv_sb[:, k, c * P:c * P + P], xt)
                if late:
                    pe.wait_ge(freed["x2t"], t2 + 1)
                    bank_free(pe, "lg", b)
                    for t in range(TB):
                        for k in range(DC):
                            last = pe.matmul(job_bank["lg"][:, t * NE:t * NE + NE], x2t[:, k, t * P:t * P + P],
                                             sel_t[:, k, :], start=(k == 0), stop=(k == DC - 1))
                    last.then_inc(done["lg"], 1)
                if front:
                    project("k", b, lambda k, c: wqkv_sb[:, k, D + c * P:D + c * P + P], xt)
                if tail:
                    attend(t1, NG - 1)
                if front:
                    project_rows("v", b, xt, lambda k: wqkv_sb[:, k, 2 * D:3 * D])
                if tail:
                    bank_free(pe, "at", b)
                    pe.wait_ge(norm_done, t1 * (2 * NG) + 2 * NG)
                    for qb in range(NQ):
                        last = pe.transpose(job_bank["at"][:, qb * P:qb * P + P], att[:, qb, :], ident[:])
                    last.then_inc(done["at"], 1)
                if front:
                    pe.wait_ge(freed["k"], b + 1)
                    score(b, 0)
                if tail:
                    pe.wait_ge(freed["at"], t1 + 1)
                    project_rows("op", b, att_t, lambda k: wo_sb[:, k, :])
                if front:
                    score(b, 1)
                    turn_probs(b, 0)
                if late:
                    bank_free(pe, "rk", b)
                    pe.wait_ge(picked_done, t2 + 1)
                    o = job_bank["rk"]
                    pe.matmul(o[:, 0:NE], earlier[:], picked[:, 0, :], start=True, stop=False)
                    pe.matmul(o[:, 0:NE], ones_bf[:], so_far[:], start=False, stop=True)
                    pe.matmul(o[:, NE:2 * NE], earlier[:], picked[:, 1, :], start=True, stop=False)
                    pe.matmul(o[:, NE:2 * NE], ones_bf[:], picked[:, 0, :], start=False, stop=False)
                    pe.matmul(o[:, NE:2 * NE], ones_bf[:], so_far[:], start=False, stop=True).then_inc(done["rk"], 1)
                for g in range(2, NG):
                    if front:
                        score(b, g)
                        turn_probs(b, g - 1)
                        attend(b, g - 2)
                    if not tail:
                        continue
                    if g == 2:
                        pe.wait_ge(x1_done, t1 * TB + TB)
                        turn("x1t", b, lambda t, c: x1[:, t, c * P:c * P + P])
                    if g == 3:
                        pe.wait_ge(freed["x1t"], t1 + 1)
                        project("cq", b, lambda k, c: wq_sb[:, k, c * P:c * P + P], x1t)
                    if g == 4:
                        bank_free(pe, "cs", b)
                        pe.wait_ge(freed["cq"], t1 * DC + DC)
                        for t in range(TB):
                            for k in range(DC):
                                last = pe.matmul(job_bank["cs"][:, t * LK:t * LK + LK], q2t[:, k, t * P:t * P + P],
                                                 k2t[:, k, bass.ds(t1 * LK, LK)], start=(k == 0), stop=(k == DC - 1))
                        last.then_inc(done["cs"], 1)
                    if g == 5:
                        bank_free(pe, "p2t", b)
                        w(pe, freed["cs"], t1 * TB + TB)
                        for t in range(TB):
                            last = pe.transpose(job_bank["p2t"][0:LK, t * P:t * P + P], p2[:, t, :], ident[:])
                        last.then_inc(done["p2t"], 1)
                    if g == 6:
                        bank_free(pe, "co", b)
                        pe.wait_ge(freed["p2t"], t1 + 1)
                        for t in range(TB):
                            last = pe.matmul(job_bank["co"][:, t * D:t * D + D], p2t[:, t, :],
                                             v2[:, bass.ds(t1, 1), :].rearrange("k a d -> k (a d)"), start=True, stop=True)
                        last.then_inc(done["co"], 1)

            round_(0, True, False, False)
            round_(1, True, True, False)
            with pe.Fori(2, B) as b:
                round_(b, True, True, True)
            round_(B, False, True, True)
            round_(B + 1, False, False, True)

            pe.wait_ge(freed["rk"], B)
            pe.wait_ge(slots_done, B)
            pe.matmul(bank_o[:, 0:NE], ones_bf[:], so_far[:], start=True, stop=True).then_inc(counted, 1)
            pe.wait_ge(table_step, TABLE_STEPS)
            pe.transpose(bank_s[0][0:1, 0:FULL], tile_col[0:FULL, 6:7], ident[0:FULL, 0:FULL])
            pe.transpose(bank_s[1][0:1, 0:FULL], tile_col[0:FULL, 7:8], ident[0:FULL, 0:FULL]).then_inc(turned, 1)
            pe.wait_ge(tables, 4)
            pe.wait_ge(experts_in, 16 * 12)

            bank_x, bank_h, bank_ht, bank_y = bank_s, bank_t, [bank_o, bank_m[0]], bank_m[1:]

            def tiles(s, par):
                if not isinstance(s, int) or s < NP2:
                    i, u = s, par
                    pe.wait_ge(xg_in[u], (s - par) * 16 + 32)
                    w(pe, gx_copied, i - 1)
                    for j in range(2):
                        for c in range(DC):
                            last = pe.transpose(bank_x[u][:, (j * DC + c) * P:(j * DC + c) * P + P],
                                                xg[u][:, j, c * P:c * P + P], ident[:])
                    last.then_inc(gx_done, 1)
                if not isinstance(s, int) or 1 <= s <= NP2:
                    i, u = s - 1, (par + 1) % 2
                    pe.wait_ge(gx_copied, i + 1)
                    w(pe, h_gated, (i - 1) * 2)
                    for j in range(2):
                        e = pe.value_load(exp_tab[0:1, bass.ds(i * 2 + j, 1)], min_val=0, max_val=NE - 1)
                        for c in range(DC):
                            last = pe.matmul(bank_h[u][:, j * ES:j * ES + ES], xgt[u][:, j, c, :],
                                             keys_sb[:, bass.ds(e, 1), c, :], start=(c == 0), stop=(c == DC - 1))
                    last.then_inc(h_done, 1)
                if not isinstance(s, int) or 2 <= s <= NP2 + 1:
                    i, u = s - 2, par
                    pe.wait_ge(h_gated, i * 2 + 2)
                    w(pe, ht_copied, i - 1)
                    for j in range(2):
                        last = pe.transpose(bank_ht[u][:, j * P:j * P + P], hr[u][:, j, :], ident[:])
                    last.then_inc(ht_done, 1)
                if not isinstance(s, int) or 3 <= s <= NP2 + 2:
                    i, u = s - 3, (par + 1) % 2
                    pe.wait_ge(ht_copied, i + 1)
                    w(pe, y_copied, i - 1)
                    for j in range(2):
                        e = pe.value_load(exp_tab[0:1, bass.ds(i * 2 + j, 1)], min_val=0, max_val=NE - 1)
                        last = pe.matmul(bank_y[u][:, j * D:j * D + D], ht[u][:, j, :],
                                         values_sb[:, bass.ds(e, 1), :], start=True, stop=True)
                    last.then_inc(y_done, 1)

            for s in range(4):
                tiles(s, s % 2)
            with pe.Fori(2, NP2 // 2) as m:
                tiles(m * 2, 0)
                tiles(m * 2 + 1, 1)
            for s in range(NP2, NP2 + 3):
                tiles(s, s % 2)

        @block.scalar
        def _(act):
            def exps(b, g):
                kw = keys_of(g // DC)[1]
                n = b * NG + g
                act.wait_ge(sub_done, n + 1)
                act.activation(pb[g % 2][:, 0:GP * kw], pb[g % 2][:, 0:GP * kw], ACT.Exp, scale=DH ** -0.5)\
                    .then_inc(exp_done, 1)

            def probs_copy(b, g):
                kw = keys_of(g // DC)[1]
                n = b * NG + g
                act.wait_ge(t_done, n + 1)
                w(act, pv_done, n - 1)
                act.activation(pt[g % 2][0:kw, :], bank_t[g % 2][0:kw, :], ACT.Copy).then_inc(pt_done, 1)

            def evict(job, t, dst, src=None):
                act.wait_ge(done[job], t + 1)
                act.activation(dst, job_bank[job][:, 0:DC * S] if src is None else src, ACT.Copy).then_inc(freed[job], 1)

            def rstd(which, t, mv, buf):
                act.wait_ge(var_done[which], t * TB + TB)
                act.activation(buf[:, 1, :], mv[:, :, 1], ACT.Ln, bias=eps_col[:]).then_inc(ln_done[which], 1)
                act.wait_ge(ln_done[which], t + 1)
                act.activation(buf[:, 2, :], buf[:, 1, :], ACT.Exp, scale=-0.5).then_inc(rstd_done[which], 1)

            def round_(b, front, tail, late):
                t1, t2 = b - 1, b - 2
                if tail:
                    probs_copy(t1, NG - 1)
                if front:
                    w(act, done["v"], b)
                    evict("xt", b, xt[:].rearrange("p c s -> p (c s)"))
                if late:
                    evict("x2t", t2, x2t[:].rearrange("p c s -> p (c s)"))
                if front:
                    w(act, s_ready, b * NG)
                    evict("q", b, qt[:].rearrange("p c s -> p (c s)"))
                if late:
                    act.wait_ge(done["lg"], t2 + 1)
                    act.activation(ex[:].rearrange("p t e -> p (t e)"), job_bank["lg"][:, 0:TB * NE], ACT.Exp, scale=-1.0)\
                        .then_inc(freed["lg"], 1)
                if tail:
                    evict("at", t1, att_t[:].rearrange("p r (n i) -> p n r i", n=NQ),
                          job_bank["at"][:].rearrange("p (n r i) -> p n r i", n=NQ, r=2))
                if front:
                    exps(b, 0)
                if tail:
                    rstd(0, t1, mv1, lnv)
                if front:
                    exps(b, 1)
                    probs_copy(b, 0)
                for g in range(2, NG):
                    if front:
                        exps(b, g)
                        probs_copy(b, g - 1)
                    if not tail:
                        continue
                    if g == 2:
                        evict("x1t", t1, x1t[:].rearrange("p c s -> p (c s)"))
                    if g == 3:
                        act.wait_ge(done["cq"], t1 + 1)
                        for c in range(DC):
                            act.activation(q2t[:, c, :], job_bank["cq"][:, c * S:c * S + S], ACT.Identity,
                                           bias=bq_sb[:, c:c + 1]).then_inc(freed["cq"], 1)
                    if g == 4:
                        act.wait_ge(cneg_done, t1 + 1)
                        for t in range(TB):
                            act.activation(p2[:, t, :], job_bank["cs"][:, t * LK:t * LK + LK], ACT.Exp,
                                           bias=cneg[:, t:t + 1], scale=D ** -0.5,
                                           accum_out=csum[:, t:t + 1]).then_inc(freed["cs"], 1)
                    if g == 5:
                        evict("p2t", t1, p2t[:].rearrange("k t p -> k (t p)"), job_bank["p2t"][0:LK, 0:TB * P])
                    if g == 6:
                        rstd(1, t1, mv2, lnv2)

            act.wait_ge(consts, 1)
            act.wait_ge(pro_ev, 13)
            round_(0, True, False, False)
            round_(1, True, True, False)
            with act.Fori(2, B) as b:
                round_(b, True, True, True)
            round_(B, False, True, True)
            round_(B + 1, False, False, True)

            def tiles(i, par, m):
                act.wait_ge(gate_kept, i + 1)
                act.wait_ge(h_done, i + 1)
                w(act, ht_done, i - 1)
                for j in range(2):
                    act.activation(hr[par][:, j, :], bank_t[par][:, j * ES:j * ES + ES], ACT.Relu,
                                   scale=gate_col[par][:, j:j + 1]).then_inc(h_gated, 1)
                act.wait_ge(ht_done, i + 1)
                w(act, y_done, i - 1)
                act.activation(ht[par][:].rearrange("p j f -> p (j f)"), [bank_o, bank_m[0]][par][:, 0:2 * P], ACT.Copy)\
                    .then_inc(ht_copied, 1)

            tiles(0, 0, 0)
            tiles(1, 1, 0)
            with act.Fori(1, NP2 // 2) as m:
                tiles(m * 2, 0, m)
                tiles(m * 2 + 1, 1, m)

            act.wait_ge(var3_done, 1)
            act.activation(ln3[:, 4, :], ln3[:, 3, :], ACT.Ln).then_inc(rstd3_done, 1)
            act.wait_ge(rstd3_done, 1)
            act.activation(ln3[:, 5, :], ln3[:, 4, :], ACT.Exp, scale=-0.5).then_inc(rstd3_done, 1)

        @block.vector
        def _(dve):
            dve.wait_ge(consts, 1)
            dve.wait_ge(weights_in, 16 * (11 + PAIRS))
            dve.wait_ge(pro_pe, 1)
            HB = B // 2
            for h in range(2):
                f = slice(h * HB * LK, (h + 1) * HB * LK)
                dve.tensor_copy(ctx_t[:, f], bank_s[h][:, 0:HB * LK]).then_inc(pro_ev, 1)
                dve.tensor_copy(ctx2_t[:, f], bank_t[h][0:TXT2, 0:HB * LK]).then_inc(pro_ev, 1)
            dve.tensor_copy(sel_t[:].rearrange("p c e -> p (c e)"), bank_o[:, 0:DC * NE]).then_inc(pro_ev, 1)
            dve.wait_ge(pro_pe, 2)
            for i in range(B // 2):
                bank = [*bank_m, bank_o][i]
                dve.tensor_tensor(out=v2[:, 2 * i:2 * i + 2, :], in0=bank[0:LK, :].rearrange("k (n d) -> k n d", n=2),
                                  in1=bv_sb[:].unsqueeze(1).broadcast_to([LK, 2, D]), op=ALU.add).then_inc(pro_ev, 1)
            dve.wait_ge(pro_pe, 3)
            for c in range(DC):
                for h in range(2):
                    dve.tensor_scalar(k2t[:, c, h * HB * LK:(h + 1) * HB * LK], [*bank_s, *bank_t][2 * c + h][:, 0:HB * LK],
                                      bk_sb[:, c:c + 1], None, ALU.add).then_inc(pro_ev, 1)

            def soft_max(b, g):
                kw = keys_of(g // DC)[1]
                n = b * NG + g
                s3 = bank_s[g % 2][:, 0:GP * kw].rearrange("p (a j) -> p a j", a=GP)
                dve.wait_ge(s_ready, n + 1)
                dve.tensor_reduce(mx[g % 2][:], s3, AX.X, ALU.max).then_inc(mx_done, 1)
                w(dve, t_done, n - 1)
                dve.wait_ge(mx_done, n + 1)
                dve.tensor_tensor(out=pb[g % 2][:, 0:GP * kw].rearrange("p (a j) -> p a j", a=GP), in0=s3,
                                  in1=mx[g % 2][:].unsqueeze(2).broadcast_to([P, GP, kw]), op=ALU.subtract)\
                    .then_inc(sub_done, 1)

            def normalise(b, g):
                qb, c = g // DC, g % DC
                n = b * NG + g
                o3 = bank_o[:, 0:GP * VC].rearrange("p (a v) -> p a v", a=GP)
                dve.wait_ge(pv_done, n + 1)
                dve.reciprocal(rs[g % 2][:], o3[:, :, 2 * DH]).then_inc(rs_done, 1)
                if g == 0:
                    w(dve, done["at"], b)
                dve.wait_ge(rs_done, n + 1)
                a3 = att[:, qb, c * GP * DH:(c + 1) * GP * DH].rearrange("p (a d) -> p a d", a=GP)
                for h in range(2):
                    q = slice(WIN * h, WIN * h + WIN)
                    dve.tensor_tensor(out=a3[q], in0=o3[q, :, h * DH:h * DH + DH],
                                      in1=rs[g % 2][q].unsqueeze(2).broadcast_to([WIN, GP, DH]), op=ALU.mult)\
                        .then_inc(norm_done, 1)

            ln1 = Steps(dve, ln1_step, TB + 4)
            ln2 = Steps(dve, ln2_step, 2 * TB + 4)
            tk = Steps(dve, topk_step, 10)
            sl = Steps(dve, slot_step, 4)

            def statistics(steps, which, r, st, mv, buf):
                for t in range(TB):
                    ins = dve.bn_stats(st[:, t, :], r[:, t, :])
                    if t == TB - 1:
                        steps.link(ins)
                    else:
                        ins.then_inc(steps.sem, 1)
                        steps.n += 1
                w(dve, steps.sem, steps.base + steps.n)
                for t in range(TB):
                    dve.bn_aggr(mv[:, t, :], st[:, t, :]).then_inc(var_done[which], 1)

            def sharpen(steps, which, t, mv, buf):
                dve.wait_ge(rstd_done[which], t + 1)
                steps.link(dve.tensor_scalar(buf[:, 0, :], mv[:, :, 1], LN_EPS, None, ALU.add))
                steps.link(dve.tensor_tensor(out=buf[:, 3, :], in0=buf[:, 2, :], in1=buf[:, 2, :], op=ALU.mult))
                steps.link(dve.scalar_tensor_tensor(out=buf[:, 4, :], in0=buf[:, 3, :], scalar=-0.5, in1=buf[:, 0, :],
                                                    op0=ALU.mult, op1=ALU.mult))
                steps.link(dve.scalar_tensor_tensor(out=buf[:, 5, :], in0=buf[:, 4, :], scalar=1.5, in1=buf[:, 2, :],
                                                    op0=ALU.add, op1=ALU.mult))

            def out_residual(t1):
                ln1.begin(t1)
                dve.wait_ge(done["op"], t1 + 1)
                dve.wait_ge(xr_in, t1 * 16 + 16)
                dve.tensor_tensor(out=r1[:].rearrange("p t d -> p (t d)"), in0=job_bank["op"][:],
                                  in1=xr[:].rearrange("p t d -> p (t d)"), op=ALU.add).then_inc(freed["op"], 1)
                dve.wait_ge(freed["op"], t1 + 1)
                statistics(ln1, 0, r1, st1, mv1, lnv)

            def layer_norm1(t1):
                sharpen(ln1, 0, t1, mv1, lnv)
                w(dve, done["x1t"], t1)
                for t in range(TB):
                    ins = dve.tensor_scalar(x1[:, t, :], r1[:, t, :], mv1[:, t, 0:1], lnv[:, 5, t:t + 1],
                                            ALU.subtract, ALU.mult)
                    ins.then_inc(x1_done, 1)
                ln1.n += 2

            def cross_max(t1):
                dve.wait_ge(done["cs"], t1 + 1)
                dve.tensor_reduce(cmx[:], job_bank["cs"][:, 0:TB * LK].rearrange("p (t k) -> p t k", t=TB), AX.X,
                                  ALU.max).then_inc(cmx_done, 1)
                dve.wait_ge(cmx_done, t1 + 1)
                dve.tensor_scalar(cneg[:], cmx[:], -(D ** -0.5), None, ALU.mult).then_inc(cneg_done, 1)

            def cross_residual(t1):
                ln2.begin(t1)
                dve.wait_ge(freed["cs"], t1 * TB + TB)
                ln2.link(dve.reciprocal(crec[:], csum[:]))
                dve.wait_ge(done["co"], t1 + 1)
                for t in range(TB):
                    ins = dve.scalar_tensor_tensor(out=r2[:, t, :], in0=job_bank["co"][:, t * D:t * D + D],
                                                   scalar=crec[:, t:t + 1], in1=x1[:, t, :], op0=ALU.mult, op1=ALU.add)
                    if t == TB - 1:
                        ins.then_inc(freed["co"], 1)
                    else:
                        ins.then_inc(ln2.sem, 1)
                        ln2.n += 1
                dve.wait_ge(freed["co"], t1 + 1)
                dve.wait_ge(ln2.sem, ln2.base + ln2.n)
                statistics(ln2, 1, r2, st2, mv2, lnv2)

            def layer_norm2(t1):
                sharpen(ln2, 1, t1, mv2, lnv2)
                w(dve, scattered, t1 * (16 * TB * TOPK))
                w(dve, x2_kept, t1 * 16)
                w(dve, done["x2t"], t1)
                for t in range(TB):
                    dve.tensor_scalar(xs[:, t, :, 0:D], r2[:, t, :].unsqueeze(1).broadcast_to([P, TOPK, D]),
                                      mv2[:, t, 0:1], lnv2[:, 5, t:t + 1], ALU.subtract, ALU.mult).then_inc(x2_done, 1)
                ln2.n += 0

            def top_experts(t2):
                tk.begin(t2)
                dve.wait_ge(freed["lg"], t2 + 1)
                tk.link(dve.tensor_scalar(ex1[:], ex[:], 1.0, None, ALU.add))
                tk.link(dve.reciprocal(gates[:], ex1[:]))
                w(dve, tk.sem, tk.base + tk.n)
                for t in range(TB):
                    ins = dve.max(top_v[:, t, :], gates[:, t, :])
                    if t == TB - 1:
                        tk.link(ins)
                    else:
                        ins.then_inc(tk.sem, 1)
                        tk.n += 1
                w(dve, tk.sem, tk.base + tk.n)
                for t in range(TB):
                    ins = dve.max_index(top_i[:, t, :], top_v[:, t, :], gates[:, t, :])
                    if t == TB - 1:
                        tk.link(ins)
                    else:
                        ins.then_inc(tk.sem, 1)
                        tk.n += 1
                tk.link(dve.tensor_copy(top_f[:], top_i[:, :, 0:TOPK]))
                tk.link(dve.tensor_tensor(out=onehot[:], in0=e_index[:],
                                          in1=top_f[:].rearrange("p t k -> p (t k)").unsqueeze(2).broadcast_to([P, TB * TOPK, NE]),
                                          op=ALU.is_equal))
                with nc.allow_low_precision("zeros and ones"):
                    dve.tensor_reduce(picked[:], onehot[:].rearrange("p (t k) e -> p t e k", t=TB), AX.X, ALU.add)\
                        .then_inc(picked_done, 1)
                dve.tensor_copy(xs[:, :, :, D + 1:D + 2], top_v[:, :, 0:TOPK].unsqueeze(3)).then_inc(tk.sem, 1)
                tk.n += 1
                tk.link(dve.tensor_copy(xs[:, :, :, D:D + 1].bitcast(I32), row_id[:].unsqueeze(3)))
                dve.tensor_scalar(row_id[:], row_id[:], S * TOPK, None, ALU.add).then_inc(row_id_done, 1)
                tk.end()

            def rows(t2):
                sl.begin(t2)
                dve.wait_ge(done["rk"], t2 + 1)
                dve.tensor_tensor(out=place[:].rearrange("p t e -> p (t e)"), in0=job_bank["rk"][:, 0:TB * NE],
                                  in1=e_start[:].rearrange("p t e -> p (t e)"), op=ALU.add).then_inc(freed["rk"], 1)
                dve.wait_ge(freed["rk"], t2 + 1)
                with nc.allow_low_precision("small whole numbers"):
                    sl.link(dve.tensor_tensor(out=so_far[:], in0=so_far[:], in1=picked[:, 0, :], op=ALU.add))
                    sl.link(dve.tensor_tensor(out=so_far[:], in0=so_far[:], in1=picked[:, 1, :], op=ALU.add))
                sl.link(dve.tensor_tensor(out=prod[:].rearrange("p (t k) e -> p t k e", t=TB),
                                          in0=onehot[:].rearrange("p (t k) e -> p t k e", t=TB),
                                          in1=place[:].unsqueeze(2).broadcast_to([P, TB, TOPK, NE]), op=ALU.mult))
                sl.link(dve.tensor_reduce(slot_f[:], prod[:], AX.X, ALU.add))
                dve.tensor_copy(slot[:], slot_f[:]).then_inc(slots_done, 1)
                sl.end()

            def round_(b, front, tail, late):
                t1, t2 = b - 1, b - 2
                if tail:
                    normalise(t1, NG - 2)
                if front:
                    dve.wait_ge(done["k"], b + 1)
                    dve.tensor_copy(kt[:].rearrange("p c s -> p (c s)"), job_bank["k"][:]).then_inc(freed["k"], 1)
                if tail:
                    normalise(t1, NG - 1)
                if late:
                    top_experts(t2)
                if front:
                    dve.wait_ge(done["v"], b + 1)
                    w(dve, vw_in, b * 32)
                    dve.tensor_copy(vw[:, 0:TB, :, 0:2 * DH],
                                    job_bank["v"][:].rearrange("p (t a v) -> p t a v", t=TB, a=PAIRS)).then_inc(freed["v"], 1)
                    soft_max(b, 0)
                if tail:
                    out_residual(t1)
                if front:
                    soft_max(b, 1)
                if tail:
                    layer_norm1(t1)
                if late:
                    rows(t2)
                for g in range(2, NG):
                    if front:
                        soft_max(b, g)
                        normalise(b, g - 2)
                    if tail and g == 4:
                        cross_max(t1)
                    if tail and g == 6:
                        cross_residual(t1)
                if tail:
                    layer_norm2(t1)

            round_(0, True, False, False)
            round_(1, True, True, False)
            with dve.Fori(2, B) as b:
                round_(b, True, True, True)
            round_(B, False, True, True)
            round_(B + 1, False, False, True)

            tb = Steps(dve, table_step, TABLE_STEPS)
            tb.begin(0)
            dve.wait_ge(counted, 1)
            tb.link(dve.tensor_copy(counts[:], bank_o[:, 0:NE]))
            dve.tensor_tensor(out=pad_tab[:], in0=counts[0:1, :], in1=e_start[0:1, 0, :], op=ALU.add).then_inc(tables, 1)
            tb.link(dve.tensor_scalar(ended_n[:], counts[:], -(P - 1) / 2, 1.0 / P, ALU.add, ALU.mult))
            tb.link(dve.tensor_scalar(fulls[:], ended_n[:], MAGIC, None, ALU.add))
            tb.link(dve.tensor_scalar(fulls[:], fulls[:], MAGIC, None, ALU.subtract))
            tb.link(dve.tensor_tensor_scan(full_end[:], fulls[:], zeros[:], 0.0, ALU.add, ALU.add))
            tb.link(dve.tensor_scalar(ended[:], full_end[:], part_no[:], None, ALU.is_le))
            tb.link(dve.tensor_reduce(tile_col[:, 0:1], ended[:], AX.X, ALU.add))
            tb.link(dve.tensor_tensor(out=ended_n[:], in0=ended[:], in1=fulls[:], op=ALU.mult))
            tb.link(dve.tensor_reduce(tile_col[:, 1:2], ended_n[:], AX.X, ALU.add))
            tb.link(dve.tensor_tensor(out=tile_col[:, 2:3], in0=part_no[:], in1=tile_col[:, 1:2], op=ALU.subtract))
            tb.link(dve.tensor_scalar(tile_col[:, 3:4], tile_col[:, 2:3], float(P), None, ALU.mult))
            tb.link(dve.tensor_scalar(tile_col[:, 4:5], tile_col[:, 0:1], float(SEG), None, ALU.mult))
            tb.link(dve.tensor_tensor(out=tile_col[:, 5:6], in0=tile_col[:, 3:4], in1=tile_col[:, 4:5], op=ALU.add))
            tb.link(dve.tensor_scalar(tile_col[:, 6:7], tile_col[:, 5:6], float(NE * SEG), None, ALU.min))
            tb.link(dve.tensor_scalar(tile_col[:, 7:8], tile_col[:, 0:1], float(NE - 1), None, ALU.min))
            tb.end()
            dve.scalar_tensor_tensor(out=row_tab[:, FULL:NTILES], in0=fulls[0:1, :], scalar=float(P), in1=e_start[0:1, 0, :],
                                     op0=ALU.mult, op1=ALU.add).then_inc(tables, 1)
            dve.wait_ge(turned, 1)
            dve.tensor_copy(row_tab[:, 0:FULL], bank_s[0][0:1, 0:FULL]).then_inc(tables, 1)
            dve.tensor_copy(exp_tab[:, 0:FULL], bank_s[1][0:1, 0:FULL]).then_inc(tables, 1)

            def tiles(s, k):
                par = k % 2
                if not isinstance(s, int) or s < NP2:
                    dve.wait_ge(xg_in[par], (s - par) * 16 + 32)
                    w(dve, y_sent[par], (s - par) * 16 - 32)
                    dve.tensor_copy(ids[k][:], xg[par][:, :, D:D + 1].bitcast(I32).rearrange("p j a -> p (j a)"))\
                        .then_inc(ids_kept, 1)
                    w(dve, h_gated, (s - 1) * 2)
                    dve.tensor_copy(gate_col[par][:], xg[par][:, :, D + 1:D + 2].rearrange("p j a -> p (j a)"))\
                        .then_inc(gate_kept, 1)
                    dve.wait_ge(gx_done, s + 1)
                    w(dve, h_done, s - 1)
                    dve.tensor_copy(xgt[par][:].rearrange("p j c f -> p (j c f)"), bank_s[par][:]).then_inc(gx_copied, 1)
                if not isinstance(s, int) or s >= 2:
                    i = s - 2
                    dve.wait_ge(y_done, i + 1)
                    w(dve, y_sent[par], (s - par) * 16 - 32)
                    dve.tensor_copy(yb[par].rearrange("p j d -> p (j d)"), bank_m[1 + par][:]).then_inc(y_copied, 1)

            for s in range(4):
                tiles(s, s)
            with dve.Fori(1, NP2 // 4) as m:
                for k in range(4):
                    tiles(m * 4 + k, k)
            for s in range(NP2, NP2 + 2):
                tiles(s, s % 4)

            def sums(t, par):
                dve.wait_ge(half_done, t + 1)
                dve.tensor_tensor(out=quarter[:], in0=half[par][:, 0, :], in1=half[par][:, 1, :], op=ALU.add).then_inc(sum_step, 1)
                dve.wait_ge(sum_step, t * 2 + 1)
                xt_ = x2_all[:, bass.ds(t, 1), :].rearrange("p a d -> p (a d)")
                dve.tensor_tensor(out=xt_, in0=quarter[:], in1=xt_, op=ALU.add).then_inc(sum_step, 1)
                dve.wait_ge(sum_step, t * 2 + 2)
                dve.bn_stats(st3[:, bass.ds(t, 1), :].rearrange("p a d -> p (a d)"), xt_).then_inc(stats_done, 1)

            dve.wait_ge(x2_kept, 16 * B)
            with dve.Fori(0, NT // 2) as m:
                sums(m * 2, 0)
                sums(m * 2 + 1, 1)
            l3 = Steps(dve, ln3_step, 9)
            l3.begin(0)
            dve.wait_ge(stats_done, NT)
            l3.link(dve.tensor_tensor(out=ln3[:, 0, :], in0=st3[:, :, 1], in1=st3[:, :, 4], op=ALU.add))
            l3.link(dve.tensor_tensor(out=ln3[:, 1, :], in0=st3[:, :, 1], in1=st3[:, :, 4], op=ALU.subtract))
            l3.link(dve.tensor_tensor(out=ln3[:, 2, :], in0=st3[:, :, 2], in1=st3[:, :, 5], op=ALU.add))
            l3.link(dve.scalar_tensor_tensor(out=ln3[:, 1, :], in0=ln3[:, 1, :], scalar=0.25, in1=ln3[:, 1, :],
                                             op0=ALU.mult, op1=ALU.mult))
            l3.link(dve.tensor_scalar(ln3[:, 2, :], ln3[:, 2, :], 1.0 / D, LN_EPS, ALU.mult, ALU.add))
            dve.tensor_tensor(out=ln3[:, 3, :], in0=ln3[:, 1, :], in1=ln3[:, 2, :], op=ALU.add).then_inc(var3_done, 1)
            l3.link(dve.tensor_scalar(ln3[:, 0, :], ln3[:, 0, :], 0.5, None, ALU.mult))
            dve.wait_ge(var3_done, 1)
            dve.wait_ge(rstd3_done, 2)
            l3.link(dve.tensor_tensor(out=ln3[:, 6, :], in0=ln3[:, 5, :], in1=ln3[:, 5, :], op=ALU.mult))
            l3.link(dve.scalar_tensor_tensor(out=ln3[:, 7, :], in0=ln3[:, 6, :], scalar=-0.5, in1=ln3[:, 3, :],
                                             op0=ALU.mult, op1=ALU.mult))
            l3.link(dve.scalar_tensor_tensor(out=ln3[:, 6, :], in0=ln3[:, 7, :], scalar=1.5, in1=ln3[:, 5, :],
                                             op0=ALU.add, op1=ALU.mult))
            l3.end()
            with dve.Fori(0, NT) as t:
                xt_ = x2_all[:, bass.ds(t, 1), :].rearrange("p a d -> p (a d)")
                dve.tensor_scalar(xt_, xt_, ln3[:, 0, bass.ds(t, 1)], ln3[:, 6, bass.ds(t, 1)],
                                  ALU.subtract, ALU.mult).then_inc(out_ready, 1)


_INS = ["x", "ctx_768", "L0_attn_W_qkv", "L0_attn_W_out", "L0_xattn_Wq", "L0_xattn_bq", "L0_xattn_Wk", "L0_xattn_bk",
        "L0_xattn_Wv", "L0_xattn_bv", "L0_ffn_expert_sel", "L0_ffn_keys", "L0_ffn_values"]


def kernel(**inputs):
    import numpy as np
    import concourse.bacc as bacc
    from concourse.bass_utils import run_bass_kernel_spmd as run

    nc = bacc.Bacc("TRN2", target_bir_lowering=False, num_devices=1)
    arrays, args = {}, []
    for name in _INS:
        a = np.ascontiguousarray(inputs[name])
        arrays[f"in_{name}"] = a
        args.append(nc.dram_tensor(f"in_{name}", a.shape, mybir.dt.from_np(a.dtype), kind="ExternalInput").ap())
    b, s, d = inputs["x"].shape
    n_experts = inputs["L0_ffn_expert_sel"].shape[0]
    out = nc.dram_tensor("out", (b, s, d), F32, kind="ExternalOutput").ap()
    rows = nc.dram_tensor("rows", (n_experts * (b * s + P) + P, d + 2), F32, kind="Internal").ap()
    parts = nc.dram_tensor("parts", (b * s * 4, d), F32, kind="Internal").ap()
    decoder_layer(nc, *args, out, rows, parts)
    r = run(nc, [arrays], core_ids=[0])
    return r.results[0]["out"]
```

```python
from contextlib import ExitStack

import concourse.bass as bass
from concourse import mybir

F32 = mybir.dt.float32
BF16 = mybir.dt.bfloat16
I32 = mybir.dt.int32
U32 = mybir.dt.uint32
ALU = mybir.AluOpType
ACT = mybir.ActivationFunctionType
AX = mybir.AxisListType

P = 128
NEG = -1.0e30
MAGIC = 12582912.0
LN_EPS = 1e-5


def decoder_layer(nc, x, ctx_in, w_qkv, w_out, wq, bq, wk, bk, wv, bv, expert_sel, keys, values, out, rows_dram, parts_dram):
    B, S, D = x.shape
    LK, TXT = ctx_in.shape[1:]
    NE, _, ES = keys.shape
    TOPK, HEADS, DH, WIN = 4, 16, 16, 64
    DC = D // P
    TB = S // P
    NT = B * TB
    PAIRS = HEADS // 2
    HC = HEADS // DC
    GP = PAIRS // DC
    NQ = S // WIN
    NG = NQ * DC
    VC = 2 * DH + 1
    TXT2 = TXT - P
    ROW = D + 2
    SEG = P + B * S
    NTILES = B * S * TOPK // P + NE
    NP2 = NTILES // 2
    RING = 4
    TABLE_STEPS = 14
    PAD_ID = 1 << 20

    with ExitStack() as stack:
        def sb(name, shape, dt=F32):
            return stack.enter_context(nc.sbuf_tensor(name, shape, dt))

        def ps(name):
            return stack.enter_context(nc.psum_tensor(name, [P, 512], F32))

        def sem(name):
            return stack.enter_context(nc.semaphore(name))

        ident = sb("ident", [P, P])
        ident_bf = sb("ident_bf", [P, P], BF16)
        mask = sb("mask", [P, GP, P], BF16)
        mask0 = sb("mask0", [P, GP, WIN], BF16)
        earlier = sb("earlier", [P, P], BF16)
        ones_bf = sb("ones_bf", [P, P], BF16)
        zeros = sb("zeros", [P, NE])
        e_index = sb("e_index", [P, TB * TOPK, NE])
        e_start = sb("e_start", [P, TB, NE])
        row_id = sb("row_id", [P, TB, TOPK], I32)
        eps_col = sb("eps_col", [P, 1])
        pad_rows = sb("pad_rows", [P, ROW])
        wqkv_sb = sb("wqkv_sb", [P, DC, 3 * D])
        wo_sb = sb("wo_sb", [P, 2, D])
        wq_sb = sb("wq_sb", [P, DC, D])
        wk_sb = sb("wk_sb", [P, D])
        wk2_sb = sb("wk2_sb", [TXT2, D])
        wv_sb = sb("wv_sb", [P, D])
        wv2_sb = sb("wv2_sb", [TXT2, D])
        bq_sb = sb("bq_sb", [P, DC])
        bk_sb = sb("bk_sb", [P, DC])
        bv_sb = sb("bv_sb", [LK, D])
        sel_rows = sb("sel_rows", [NE, D])
        sel_t = sb("sel_t", [P, DC, NE])
        keys_sb = sb("keys_sb", [P, NE, DC, ES])
        values_sb = sb("values_sb", [P, NE, D])
        ctx_sb = sb("ctx_sb", [LK, B, TXT])
        ctx_t = sb("ctx_t", [P, B * LK])
        ctx2_t = sb("ctx2_t", [TXT2, B * LK])
        k2t = sb("k2t", [P, DC, B * LK])
        v2 = sb("v2", [LK, B, D])
        xf = sb("xf", [P, TB, D])
        xr = sb("xr", [P, TB, D])
        xt = sb("xt", [P, DC, S])
        qt = sb("qt", [P, DC, S])
        qx = sb("qx", [P, DC * NQ, HC, WIN])
        kt = sb("kt", [P, DC, S])
        vw = sb("vw", [P, 3, PAIRS, VC])
        pb = [sb(f"pb{i}", [P, GP * P]) for i in range(2)]
        pt = [sb(f"pt{i}", [P, GP * P]) for i in range(2)]
        mx = [sb(f"mx{i}", [P, GP]) for i in range(2)]
        rs = [sb(f"rs{i}", [P, GP]) for i in range(2)]
        att = sb("att", [P, NQ, P])
        att_t = sb("att_t", [P, 2, S])
        r1 = sb("r1", [P, TB, D])
        x1 = sb("x1", [P, TB, D])
        x1t = sb("x1t", [P, DC, S])
        st1 = sb("st1", [P, TB, 6])
        mv1 = sb("mv1", [P, TB, 2])
        lnv = sb("lnv", [P, 6, TB])
        st2 = sb("st2", [P, TB, 6])
        mv2 = sb("mv2", [P, TB, 2])
        lnv2 = sb("lnv2", [P, 6, TB])
        q2t = sb("q2t", [P, DC, S])
        cmx = sb("cmx", [P, TB])
        cneg = sb("cneg", [P, TB])
        csum = sb("csum", [P, TB])
        crec = sb("crec", [P, TB])
        p2 = sb("p2", [P, TB, LK])
        p2t = sb("p2t", [LK, TB, P])
        r2 = sb("r2", [P, TB, D])
        xs = sb("xs", [P, TB, TOPK, ROW])
        x2t = sb("x2t", [P, DC, S])
        ex = sb("ex", [P, TB, NE])
        ex1 = sb("ex1", [P, TB, NE])
        gates = sb("gates", [P, TB, NE])
        top_v = sb("top_v", [P, TB, 8])
        top_i = sb("top_i", [P, TB, 8], U32)
        top_f = sb("top_f", [P, TB, TOPK])
        onehot = sb("onehot", [P, TB * TOPK, NE])
        picked = sb("picked", [P, TB, NE], BF16)
        so_far = sb("so_far", [P, NE], BF16)
        place = sb("place", [P, TB, NE])
        prod = sb("prod", [P, TB * TOPK, NE])
        slot_f = sb("slot_f", [P, TB * TOPK])
        slot = sb("slot", [P, TB * TOPK], U32)
        x2_all = sb("x2_all", [P, NT, D])

        bank_s = [ps(f"bank_s{i}") for i in range(2)]
        bank_t = [ps(f"bank_t{i}") for i in range(2)]
        bank_o = ps("bank_o")
        bank_m = [ps(f"bank_m{i}") for i in range(3)]

        JOBS = ["xt", "x2t", "q", "lg", "k", "v", "at", "op", "rk", "x1t", "cq", "cs", "p2t", "co"]
        LATE = {**{j: 0 for j in ("xt", "q", "k", "v")},
                **{j: 1 for j in ("at", "op", "x1t", "cq", "cs", "p2t", "co")},
                **{j: 2 for j in ("x2t", "lg", "rk")}}
        job_bank = {j: bank_m[n % 3] for n, j in enumerate(JOBS)}
        done = {j: sem("pe_" + j) for j in JOBS}
        freed = {j: sem("free_" + j) for j in JOBS}

        weights_in = sem("weights_in")
        experts_in = sem("experts_in")
        consts = sem("consts")
        chain_p = sem("chain_p")
        ln1_step = sem("ln1_step")
        ln2_step = sem("ln2_step")
        topk_step = sem("topk_step")
        slot_step = sem("slot_step")
        ln3_step = sem("ln3_step")
        stats_done = sem("stats_done")
        row_id_done = sem("row_id_done")
        cmx_done = sem("cmx_done")
        ln_done = [sem("ln1_log"), sem("ln2_log")]
        pro_pe = sem("pro_pe")
        pro_ev = sem("pro_ev")
        xf_in = sem("xf_in")
        xr_in = sem("xr_in")
        qx_in = [sem(f"qx_in{i}") for i in range(GP)]
        vw_in = sem("vw_in")
        s_ready = sem("s_ready")
        mx_done = sem("mx_done")
        sub_done = sem("sub_done")
        exp_done = sem("exp_done")
        t_done = sem("t_done")
        pt_done = sem("pt_done")
        pv_done = sem("pv_done")
        rs_done = sem("rs_done")
        norm_done = sem("norm_done")
        var_done = [sem("var1_done"), sem("var2_done")]
        rstd_done = [sem("rstd1_done"), sem("rstd2_done")]
        x1_done = sem("x1_done")
        x2_done = sem("x2_done")
        x2_kept = sem("x2_kept")
        cneg_done = sem("cneg_done")
        p2_done = sem("p2_done")
        picked_done = sem("picked_done")
        slots_done = sem("slots_done")
        scattered = sem("scattered")
        pads_in = sem("pads_in")
        out_in = sem("out_in")

        def room(t, at, shape):
            flat = t[:].rearrange("p a b -> p (a b)")[:, at:at + shape[0] * shape[1]]
            return flat.rearrange("p (a b) -> p a b", a=shape[0])

        xg = [sb(f"xg{i}", [P, 2, ROW])[:] for i in range(2)] + [room(wqkv_sb, i * 2 * ROW, (2, ROW)) for i in range(2)]
        id_gate = [sb(f"id_gate{i}", [P, 2, 2]) for i in range(RING)]
        xgt = [sb(f"xgt{i}", [P, 2, DC, P]) for i in range(2)]
        expert_keys = [xt, qt]
        ht = [sb(f"ht{i}", [P, 2, P]) for i in range(2)]
        spare = qx[:].rearrange("p n h q -> p (n h q)")
        yb = [spare[:, i * 2 * D:(i + 1) * 2 * D].rearrange("p (j d) -> p j d", j=2) for i in range(RING)]
        tiles_of = sb("tiles_of", [P, NE])
        tiles_end = sb("tiles_end", [P, NE])
        tile_at = sb("tile_at", [P, NE])
        ended = sb("ended", [P, NE])
        its_expert = sb("its_expert", [P, NE])
        tile_row = sb("tile_row", [P, NE])
        tile_exp = sb("tile_exp", [P, NE])
        tile_no = sb("tile_no", [P, 2])
        tile_col = sb("tile_col", [P, 2])
        row_tab = sb("row_tab", [1, NTILES], I32)
        exp_tab = sb("exp_tab", [1, NTILES], I32)
        counted = sem("counted")
        turned = sem("turned")
        tables = sem("tables")
        table_step = sem("table_step")
        xg_in = [sem(f"xg_in{i}") for i in range(RING)]
        ids_kept = sem("ids_kept")
        keys_ready = sem("keys_ready")
        gx_done = sem("gx_done")
        gx_copied = sem("gx_copied")
        h_done = sem("h_done")
        h_ready = sem("h_ready")
        y_done = sem("y_done")
        y_copied = sem("y_copied")
        y_sent = [sem(f"y_sent{i}") for i in range(RING)]
        PR = 4
        QT = 4
        parts_sb = [spare[:, i * TOPK * D:(i + 1) * TOPK * D].rearrange("p (k d) -> p k d", k=TOPK) for i in range(PR)]
        half = [kt, r1]
        quarter = [sb(f"quarter{i}", [P, D]) for i in range(2)]
        st3 = sb("st3", [P, NT, 6])
        ln3 = sb("ln3", [P, 8, NT])
        mean3 = sb("mean3", [P, NT])
        parts_in = [sem(f"parts_in{i}") for i in range(PR)]
        half_done = sem("half_done")
        sum_step = sem("sum_step")
        var3_done = sem("var3_done")
        rstd3_done = sem("rstd3_done")
        mean3_done = sem("mean3_done")
        out_ready = sem("out_ready")

        passed = {}

        def w(eng, s, n):
            if not isinstance(n, int) or n > 0:
                eng.wait_ge(s, n)
            if not isinstance(n, int):
                eng.sem_inc(passed[eng_name(eng)], 1)

        def eng_name(eng):
            return str(eng.engine)

        def bank_free(eng, job, b):
            n = JOBS.index(job)
            last = JOBS[n - 3] if n >= 3 else JOBS[{0: 12, 1: 13, 2: 11}[n]]
            count = b - LATE[last] + (1 if n >= 3 else 0)
            w(eng, freed[last], min(count, B) if isinstance(b, int) else count)

        class Steps:
            def __init__(self, eng, s, per):
                self.eng, self.sem, self.per = eng, s, per

            def begin(self, b):
                self.base, self.n = b * self.per, 0

            def link(self, ins):
                self.n += 1
                ins.then_inc(self.sem, 1)
                self.eng.wait_ge(self.sem, self.base + self.n)

            def end(self):
                assert self.n == self.per, (self.n, self.per)

        def keys_of(qb):
            return (0, WIN) if qb == 0 else (WIN * (qb - 1), P)

        for e in (nc.tensor, nc.vector, nc.scalar, nc.gpsimd, nc.sync):
            passed[eng_name(e)] = sem("passed_" + eng_name(e).split(".")[-1])

        block = stack.enter_context(nc.Block())

        @block.sync
        def _(sp):
            def x_of(b):
                return x[bass.ds(b, 1)].rearrange("a (t p) d -> p (a t) d", p=P)

            sp.dma_start(xf[:], x_of(0)).then_inc(xf_in, 16)
            sp.dma_start(wqkv_sb[:], w_qkv.rearrange("(c p) n -> p c n", p=P)).then_inc(weights_in, 16)
            sp.dma_start(ctx_sb[:], ctx_in.rearrange("b k t -> k b t")).then_inc(weights_in, 16)
            sp.dma_start(wk_sb[:], wk[0:P, :]).then_inc(weights_in, 16)
            sp.dma_start(wk2_sb[:], wk[P:TXT, :]).then_inc(weights_in, 16)
            sp.dma_start(wv_sb[:], wv[0:P, :]).then_inc(weights_in, 16)
            sp.dma_start(wv2_sb[:], wv[P:TXT, :]).then_inc(weights_in, 16)
            sp.dma_start(bk_sb[:], bk.rearrange("(c p) -> p c", p=P), allow_slow_non_contiguous=True).then_inc(weights_in, 16)
            sp.dma_start(bq_sb[:], bq.rearrange("(c p) -> p c", p=P), allow_slow_non_contiguous=True).then_inc(weights_in, 16)
            sp.dma_start(bv_sb[:], bv.partition_broadcast(LK)).then_inc(weights_in, 16)
            sp.dma_start(sel_rows[:], expert_sel).then_inc(weights_in, 16)
            sp.dma_start(wq_sb[:], wq.rearrange("(c p) n -> p c n", p=P)).then_inc(weights_in, 16)
            w_heads = w_out.rearrange("(a r d) n -> a d r n", r=2, d=DH)
            for a in range(PAIRS):
                sp.dma_start(wo_sb[DH * a:DH * a + DH], w_heads[a]).then_inc(weights_in, 16)
            sp.dma_start(xr[:], x_of(0)).then_inc(xr_in, 16)

            def spread(b):
                w(sp, freed["q"], b + 1)
                w(sp, s_ready, NG * b)
                for j in range(HC):
                    sp.dma_start(qx[DH * j:DH * j + DH, :, j, :],
                                 qt[DH * j:DH * j + DH, :, :].rearrange("p c (n q) -> p (c n) q", q=WIN)).then_inc(qx_in[j // 2], 16)
                w(sp, freed["v"], b + 1)
                sp.dma_start(vw[0:WIN, 2], vw[WIN:P, 0]).then_inc(vw_in, 16)
                sp.dma_start(vw[WIN:P, 2], vw[0:WIN, 1]).then_inc(vw_in, 16)

            def next_x(b):
                w(sp, done["xt"], b)
                sp.dma_start(xf[:], x_of(b)).then_inc(xf_in, 16)

            def next_residual(b):
                w(sp, freed["op"], b)
                sp.dma_start(xr[:], x_of(b)).then_inc(xr_in, 16)

            def keep_x2(b):
                w(sp, x2_done, TB * (b + 1))
                sp.dma_start(x2_all[:, bass.ds(b * TB, TB), :], xs[:, :, 0, 0:D]).then_inc(x2_kept, 16)

            next_x(1)
            spread(0)
            n = NE // 4
            for i in range(4):
                for c in range(DC):
                    sp.dma_start(keys_sb[:, n * i:n * i + n, c, :],
                                 keys[n * i:n * i + n, c * P:c * P + P, :].rearrange("e p f -> p e f")).then_inc(experts_in, 16)
                sp.dma_start(values_sb[:, n * i:n * i + n, :],
                             values[n * i:n * i + n].rearrange("e f v -> f e v")).then_inc(experts_in, 16)
            w(sp, consts, 1)
            sp.dma_start(rows_dram.rearrange("(e r) d -> r e d", e=NE)[0:P], pad_rows[:].unsqueeze(1).broadcast_to([P, NE, ROW]))\
                .then_inc(pads_in, 16)
            with sp.Fori(1, B - 1) as b:
                next_x(b + 1)
                spread(b)
                next_residual(b)
                keep_x2(b - 1)
            spread(B - 1)
            next_residual(B - 1)
            keep_x2(B - 2)
            keep_x2(B - 1)

            w(sp, pads_in, 16)
            w(sp, tables, 2)
            w(sp, scattered, 16 * TB * TOPK * B)

            def rows_of(i, k):
                w(sp, gx_done, i - RING + 1)
                w(sp, ids_kept, i - RING + 1)
                for j in range(2):
                    r = sp.value_load(row_tab[0:1, bass.ds(i * 2 + j, 1)], min_val=0, max_val=(NE - 1) * SEG + SEG - P)
                    sp.dma_start(xg[k][:, j, :], rows_dram[bass.ds(r, P), :]).then_inc(xg_in[k], 16)

            for k in range(RING):
                rows_of(k, k)
            with sp.Fori(1, NP2 // RING) as m:
                for k in range(RING):
                    rows_of(m * RING + k, k)

            for k in range(RING):
                w(sp, y_sent[k], 32 * (NP2 // RING))
            parts = parts_dram.rearrange("(t p k) d -> t p k d", p=P, k=TOPK)

            def parts_of(t, k):
                w(sp, half_done, t - PR + 1)
                sp.dma_start(parts_sb[k], parts[bass.ds(t, 1)].rearrange("a p k d -> (a p) k d")).then_inc(parts_in[k], 16)

            for k in range(PR):
                parts_of(k, k)
            with sp.Fori(1, NT // PR) as m:
                for k in range(PR):
                    parts_of(m * PR + k, k)
            out_tiles = out.rearrange("b (t p) d -> p (b t) d", p=P)
            for q in range(NT // QT):
                w(sp, out_ready, QT * (q + 1))
                sp.dma_start(out_tiles[:, QT * q:QT * q + QT, :], x2_all[:, QT * q:QT * q + QT, :]).then_inc(out_in, 16)
            w(sp, out_in, 16 * (NT // QT))

        @block.gpsimd
        def _(pool):
            count = [0]

            def link(ins):
                count[0] += 1
                ins.then_inc(chain_p, 1)
                w(pool, chain_p, count[0])

            link(pool.memset(ident[:], 0.0))
            link(pool.affine_select(out=ident[:], in_=ident[:], compare_op=ALU.not_equal, fill=1.0, base=0,
                                    pattern=[[-1, P]], channel_multiplier=1))
            link(pool.memset(ident_bf[:], 0.0))
            link(pool.affine_select(out=ident_bf[:], in_=ident_bf[:], compare_op=ALU.not_equal, fill=1.0, base=0,
                                    pattern=[[-1, P]], channel_multiplier=1))
            link(pool.memset(qx[:], 0.0))
            link(pool.memset(vw[:, :, :, 2 * DH:VC], 1.0))
            link(pool.memset(mask[:], 0.0))
            link(pool.memset(mask0[:], 0.0))
            for h in range(2):
                q = slice(WIN * h, WIN * h + WIN)
                link(pool.affine_select(out=mask[q], in_=mask[q], compare_op=ALU.is_gt, fill=NEG, base=0,
                                        pattern=[[0, GP], [1, P]], channel_multiplier=-1))
                link(pool.affine_select(out=mask[q], in_=mask[q], compare_op=ALU.is_ge, fill=NEG, base=WIN,
                                        pattern=[[0, GP], [-1, P]], channel_multiplier=1))
                link(pool.affine_select(out=mask0[q], in_=mask0[q], compare_op=ALU.is_ge, fill=NEG, base=0,
                                        pattern=[[0, GP], [-1, WIN]], channel_multiplier=1))
            link(pool.memset(ones_bf[:], 1.0))
            link(pool.memset(earlier[:], 1.0))
            link(pool.affine_select(out=earlier[:], in_=earlier[:], compare_op=ALU.is_gt, fill=0.0, base=0,
                                    pattern=[[1, P]], channel_multiplier=-1))
            link(pool.memset(zeros[:], 0.0))
            link(pool.memset(so_far[:], 0.0))
            link(pool.memset(eps_col[:], LN_EPS))
            link(pool.iota(e_index[:], pattern=[[0, TB * TOPK], [1, NE]], base=0, channel_multiplier=0,
                           allow_small_or_imprecise_dtypes=True))
            link(pool.iota(e_start[:], pattern=[[0, TB], [SEG, NE]], base=P, channel_multiplier=0,
                           allow_small_or_imprecise_dtypes=True))
            link(pool.iota(row_id[:], pattern=[[P * TOPK, TB], [1, TOPK]], base=0, channel_multiplier=TOPK))
            link(pool.iota(tile_no[:, 0:1], pattern=[[0, 1]], base=0, channel_multiplier=1,
                           allow_small_or_imprecise_dtypes=True))
            link(pool.iota(tile_no[:, 1:2], pattern=[[0, 1]], base=0, channel_multiplier=P,
                           allow_small_or_imprecise_dtypes=True))
            link(pool.memset(pad_rows[:], 0.0))
            pool.iota(pad_rows[:, D:D + 1].bitcast(I32), pattern=[[0, 1]], base=PAD_ID, channel_multiplier=0)\
                .then_inc(consts, 1)

            def scatter(b):
                w(pool, slots_done, b + 1)
                for t in range(TB):
                    for k in range(TOPK):
                        n = t * TOPK + k
                        pool.indirect_dma_start(rows_dram, bass.IndirectOffsetOnAxis(ap=slot[:, n:n + 1], axis=0),
                                                xs[:, t, k, :], None).then_inc(scattered, 16)

            with pool.Fori(0, B) as b:
                scatter(b)

            def send(i, k):
                w(pool, y_copied, i + 1)
                for j in range(2):
                    pool.indirect_dma_start(parts_dram, bass.IndirectOffsetOnAxis(ap=id_gate[k][:, j, 0:1].bitcast(U32), axis=0),
                                            yb[k][:, j, :], None, bounds_check=B * S * TOPK - 1,
                                            oob_is_err=False).then_inc(y_sent[k], 16)

            with pool.Fori(0, NP2 // RING) as m:
                for k in range(RING):
                    send(m * RING + k, k)

            def halves(t, k, m):
                w(pool, parts_in[k], m * 16 + 16)
                w(pool, sum_step, (t - 1) * 2)
                pool.tensor_tensor(out=half[k % 2][:], in0=parts_sb[k][:, 0:2, :], in1=parts_sb[k][:, 2:4, :],
                                   op=ALU.add).then_inc(half_done, 1)

            for k in range(PR):
                halves(k, k, 0)
            with pool.Fori(1, NT // PR) as m:
                for k in range(PR):
                    halves(m * PR + k, k, m)

        @block.tensor
        def _(pe):
            pe.wait_ge(consts, 1)
            pe.wait_ge(weights_in, 16 * (11 + PAIRS))
            HB = B // 2
            for h in range(2):
                for i in range(HB):
                    n = h * HB + i
                    pe.transpose(bank_s[h][:, i * LK:i * LK + LK], ctx_sb[:, n, 0:P], ident[0:LK, 0:LK])
                    last = pe.transpose(bank_t[h][0:TXT2, i * LK:i * LK + LK], ctx_sb[:, n, P:TXT], ident[0:LK, 0:LK])
            for c in range(DC):
                last = pe.transpose(bank_o[:, c * NE:c * NE + NE], sel_rows[:, c * P:c * P + P], ident[0:NE, 0:NE])
            last.then_inc(pro_pe, 1)
            pe.wait_ge(pro_ev, 5)
            for n in range(B):
                bank = [*bank_m, bank_o][n // 2]
                o = bank[0:LK, n % 2 * D:n % 2 * D + D]
                pe.matmul(o, ctx_t[:, n * LK:n * LK + LK], wv_sb[:], start=True, stop=False)
                last = pe.matmul(o, ctx2_t[:, n * LK:n * LK + LK], wv2_sb[:], start=False, stop=True)
            last.then_inc(pro_pe, 1)
            for c in range(DC):
                for h in range(2):
                    bank = [*bank_s, *bank_t][2 * c + h]
                    o = bank[:, 0:HB * LK]
                    f = slice(h * HB * LK, (h + 1) * HB * LK)
                    pe.matmul(o, wk_sb[:, c * P:c * P + P], ctx_t[:, f], start=True, stop=False)
                    last = pe.matmul(o, wk2_sb[:, c * P:c * P + P], ctx2_t[:, f], start=False, stop=True)
            last.then_inc(pro_pe, 1)
            pe.wait_ge(pro_ev, 13)

            def turn(job, b, src):
                bank_free(pe, job, b)
                for c in range(DC):
                    for t in range(TB):
                        o = job_bank[job][:, c * S + t * P:c * S + t * P + P]
                        last = pe.transpose(o, src(t, c), ident[:])
                last.then_inc(done[job], 1)

            def project(job, b, weights, src):
                bank_free(pe, job, b)
                for c in range(DC):
                    for k in range(DC):
                        last = pe.matmul(job_bank[job][:, c * S:c * S + S], weights(k, c), src[:, k, :],
                                         start=(k == 0), stop=(k == DC - 1))
                last.then_inc(done[job], 1)

            def project_rows(job, b, src, weights):
                bank_free(pe, job, b)
                for t in range(TB):
                    for k in range(DC):
                        last = pe.matmul(job_bank[job][:, t * D:t * D + D], src[:, k, t * P:t * P + P], weights(k),
                                         start=(k == 0), stop=(k == DC - 1))
                last.then_inc(done[job], 1)

            def score(b, g):
                qb, c = g // DC, g % DC
                k0, kw = keys_of(qb)
                n = b * NG + g
                o = bank_s[g % 2]
                w(pe, sub_done, n - 1)
                pe.matmul(o[:, 0:GP * kw], ident_bf[:], (mask0 if qb == 0 else mask)[:].rearrange("p a j -> p (a j)"),
                          start=True, stop=False, skip_group_check=True)
                for a in range(GP):
                    if g == 0:
                        pe.wait_ge(qx_in[a], b * 32 + 32)
                    last = pe.matmul(o[:, a * kw:a * kw + kw], qx[:, c * NQ + qb, 2 * a:2 * a + 2, :].rearrange("p h q -> p (h q)"),
                                     kt[:, c, k0:k0 + kw], start=False, stop=True, skip_group_check=True)
                last.then_inc(s_ready, 1)

            def turn_probs(b, g):
                kw = keys_of(g // DC)[1]
                n = b * NG + g
                pe.wait_ge(exp_done, n + 1)
                w(pe, pt_done, n - 1)
                for a in range(GP):
                    last = pe.transpose(bank_t[g % 2][0:kw, a * P:a * P + P], pb[g % 2][:, a * kw:a * kw + kw], ident[:])
                last.then_inc(t_done, 1)

            def attend(b, g):
                qb, c = g // DC, g % DC
                kw = keys_of(qb)[1]
                n = b * NG + g
                window = [0, 0, 2, 1][qb]
                pe.wait_ge(pt_done, n + 1)
                w(pe, norm_done, 2 * n)
                if g == 0:
                    pe.wait_ge(freed["v"], b + 1)
                if g == 2 * DC:
                    pe.wait_ge(vw_in, b * 32 + 32)
                for a in range(GP):
                    last = pe.matmul(bank_o[:, a * VC:a * VC + VC], pt[g % 2][0:kw, a * P:a * P + P],
                                     vw[0:kw, window, c * GP + a, :], start=True, stop=True)
                last.then_inc(pv_done, 1)

            def round_(b, front, tail, late):
                t1, t2 = b - 1, b - 2
                if tail:
                    turn_probs(t1, NG - 1)
                if front:
                    pe.wait_ge(xf_in, b * 16 + 16)
                    turn("xt", b, lambda t, c: xf[:, t, c * P:c * P + P])
                if late:
                    pe.wait_ge(x2_done, t2 * TB + TB)
                    turn("x2t", b, lambda t, c: xs[:, t, 0, c * P:c * P + P])
                if tail:
                    attend(t1, NG - 2)
                if front:
                    pe.wait_ge(freed["xt"], b + 1)
                    project("q", b, lambda k, c: wqkv_sb[:, k, c * P:c * P + P], xt)
                if late:
                    pe.wait_ge(freed["x2t"], t2 + 1)
                    bank_free(pe, "lg", b)
                    for t in range(TB):
                        for k in range(DC):
                            last = pe.matmul(job_bank["lg"][:, t * NE:t * NE + NE], x2t[:, k, t * P:t * P + P],
                                             sel_t[:, k, :], start=(k == 0), stop=(k == DC - 1))
                    last.then_inc(done["lg"], 1)
                if front:
                    project("k", b, lambda k, c: wqkv_sb[:, k, D + c * P:D + c * P + P], xt)
                if tail:
                    attend(t1, NG - 1)
                if front:
                    project_rows("v", b, xt, lambda k: wqkv_sb[:, k, 2 * D:3 * D])
                if tail:
                    bank_free(pe, "at", b)
                    pe.wait_ge(norm_done, t1 * (2 * NG) + 2 * NG)
                    for qb in range(NQ):
                        last = pe.transpose(job_bank["at"][:, qb * P:qb * P + P], att[:, qb, :], ident[:])
                    last.then_inc(done["at"], 1)
                if front:
                    pe.wait_ge(freed["k"], b + 1)
                    score(b, 0)
                if tail:
                    pe.wait_ge(freed["at"], t1 + 1)
                    project_rows("op", b, att_t, lambda k: wo_sb[:, k, :])
                if front:
                    score(b, 1)
                    turn_probs(b, 0)
                if late:
                    bank_free(pe, "rk", b)
                    pe.wait_ge(picked_done, t2 + 1)
                    o = job_bank["rk"]
                    pe.matmul(o[:, 0:NE], earlier[:], picked[:, 0, :], start=True, stop=False)
                    pe.matmul(o[:, 0:NE], ones_bf[:], so_far[:], start=False, stop=True)
                    pe.matmul(o[:, NE:2 * NE], earlier[:], picked[:, 1, :], start=True, stop=False)
                    pe.matmul(o[:, NE:2 * NE], ones_bf[:], picked[:, 0, :], start=False, stop=False)
                    pe.matmul(o[:, NE:2 * NE], ones_bf[:], so_far[:], start=False, stop=True).then_inc(done["rk"], 1)
                for g in range(2, NG):
                    if front:
                        score(b, g)
                        turn_probs(b, g - 1)
                        attend(b, g - 2)
                    if not tail:
                        continue
                    if g == 2:
                        pe.wait_ge(x1_done, t1 * TB + TB)
                        turn("x1t", b, lambda t, c: x1[:, t, c * P:c * P + P])
                    if g == 3:
                        pe.wait_ge(freed["x1t"], t1 + 1)
                        project("cq", b, lambda k, c: wq_sb[:, k, c * P:c * P + P], x1t)
                    if g == 4:
                        bank_free(pe, "cs", b)
                        pe.wait_ge(freed["cq"], t1 * DC + DC)
                        for t in range(TB):
                            for k in range(DC):
                                last = pe.matmul(job_bank["cs"][:, t * LK:t * LK + LK], q2t[:, k, t * P:t * P + P],
                                                 k2t[:, k, bass.ds(t1 * LK, LK)], start=(k == 0), stop=(k == DC - 1))
                        last.then_inc(done["cs"], 1)
                    if g == 5:
                        bank_free(pe, "p2t", b)
                        w(pe, freed["cs"], t1 * TB + TB)
                        for t in range(TB):
                            last = pe.transpose(job_bank["p2t"][0:LK, t * P:t * P + P], p2[:, t, :], ident[:])
                        last.then_inc(done["p2t"], 1)
                    if g == 6:
                        bank_free(pe, "co", b)
                        pe.wait_ge(freed["p2t"], t1 + 1)
                        for t in range(TB):
                            last = pe.matmul(job_bank["co"][:, t * D:t * D + D], p2t[:, t, :],
                                             v2[:, bass.ds(t1, 1), :].rearrange("k a d -> k (a d)"), start=True, stop=True)
                        last.then_inc(done["co"], 1)

            round_(0, True, False, False)
            round_(1, True, True, False)
            with pe.Fori(2, B) as b:
                round_(b, True, True, True)
            round_(B, False, True, True)
            round_(B + 1, False, False, True)

            pe.wait_ge(freed["rk"], B)
            pe.wait_ge(slots_done, B)
            pe.matmul(bank_o[:, 0:NE], ones_bf[:], so_far[:], start=True, stop=True).then_inc(counted, 1)
            pe.wait_ge(table_step, TABLE_STEPS)
            pe.transpose(bank_s[0][0:1, 0:NTILES], tile_col[0:NTILES, 0:1], ident[0:NTILES, 0:NTILES])
            pe.transpose(bank_s[1][0:1, 0:NTILES], tile_col[0:NTILES, 1:2], ident[0:NTILES, 0:NTILES]).then_inc(turned, 1)
            pe.wait_ge(tables, 2)
            pe.wait_ge(experts_in, 16 * 12)

            bank_x, bank_h, bank_y = bank_s, bank_t, bank_m[1:]

            def tiles(s, k):
                if not isinstance(s, int) or s < NP2:
                    i, u = s, k % 2
                    pe.wait_ge(xg_in[k], (s - k) * 8 + 32)
                    w(pe, gx_copied, i - 1)
                    for j in range(2):
                        for c in range(DC):
                            last = pe.transpose(bank_x[u][:, (j * DC + c) * P:(j * DC + c) * P + P],
                                                xg[k][:, j, c * P:c * P + P], ident[:])
                    last.then_inc(gx_done, 1)
                if not isinstance(s, int) or 1 <= s <= NP2:
                    i, u = s - 1, (k + 1) % 2
                    pe.wait_ge(gx_copied, i + 1)
                    pe.wait_ge(keys_ready, i + 1)
                    w(pe, h_ready, i - 1)
                    for j in range(2):
                        for c in range(DC):
                            last = pe.matmul(bank_h[u][:, j * P:j * P + P],
                                             expert_keys[u][:].rearrange("p j (c f) -> p j c f", c=DC)[:, j, c, :],
                                             xgt[u][:, j, c, :], start=(c == 0), stop=(c == DC - 1))
                    last.then_inc(h_done, 1)
                if not isinstance(s, int) or 2 <= s <= NP2 + 1:
                    i, u = s - 2, k % 2
                    pe.wait_ge(h_ready, i + 1)
                    w(pe, y_copied, i - 1)
                    for j in range(2):
                        e = pe.value_load(exp_tab[0:1, bass.ds(i * 2 + j, 1)], min_val=0, max_val=NE - 1)
                        last = pe.matmul(bank_y[u][:, j * D:j * D + D], ht[u][:, j, :],
                                         values_sb[:, bass.ds(e, 1), :], start=True, stop=True)
                    last.then_inc(y_done, 1)

            for s in range(RING):
                tiles(s, s)
            with pe.Fori(1, NP2 // RING) as m:
                for k in range(RING):
                    tiles(m * RING + k, k)
            for s in range(NP2, NP2 + 2):
                tiles(s, s % RING)

        @block.scalar
        def _(act):
            def exps(b, g):
                kw = keys_of(g // DC)[1]
                n = b * NG + g
                act.wait_ge(sub_done, n + 1)
                act.activation(pb[g % 2][:, 0:GP * kw], pb[g % 2][:, 0:GP * kw], ACT.Exp, scale=DH ** -0.5)\
                    .then_inc(exp_done, 1)

            def probs_copy(b, g):
                kw = keys_of(g // DC)[1]
                n = b * NG + g
                act.wait_ge(t_done, n + 1)
                w(act, pv_done, n - 1)
                act.activation(pt[g % 2][0:kw, :], bank_t[g % 2][0:kw, :], ACT.Copy).then_inc(pt_done, 1)

            def evict(job, t, dst, src=None):
                act.wait_ge(done[job], t + 1)
                act.activation(dst, job_bank[job][:, 0:DC * S] if src is None else src, ACT.Copy).then_inc(freed[job], 1)

            def rstd(which, t, mv, buf):
                act.wait_ge(var_done[which], t * TB + TB)
                act.activation(buf[:, 1, :], mv[:, :, 1], ACT.Ln, bias=eps_col[:]).then_inc(ln_done[which], 1)
                act.wait_ge(ln_done[which], t + 1)
                act.activation(buf[:, 2, :], buf[:, 1, :], ACT.Exp, scale=-0.5).then_inc(rstd_done[which], 1)

            def round_(b, front, tail, late):
                t1, t2 = b - 1, b - 2
                if tail:
                    probs_copy(t1, NG - 1)
                if front:
                    w(act, done["v"], b)
                    evict("xt", b, xt[:].rearrange("p c s -> p (c s)"))
                if late:
                    evict("x2t", t2, x2t[:].rearrange("p c s -> p (c s)"))
                if front:
                    w(act, s_ready, b * NG)
                    evict("q", b, qt[:].rearrange("p c s -> p (c s)"))
                if late:
                    act.wait_ge(done["lg"], t2 + 1)
                    act.activation(ex[:].rearrange("p t e -> p (t e)"), job_bank["lg"][:, 0:TB * NE], ACT.Exp, scale=-1.0)\
                        .then_inc(freed["lg"], 1)
                if tail:
                    evict("at", t1, att_t[:].rearrange("p r (n i) -> p n r i", n=NQ),
                          job_bank["at"][:].rearrange("p (n r i) -> p n r i", n=NQ, r=2))
                if front:
                    exps(b, 0)
                if tail:
                    rstd(0, t1, mv1, lnv)
                if front:
                    exps(b, 1)
                    probs_copy(b, 0)
                for g in range(2, NG):
                    if front:
                        exps(b, g)
                        probs_copy(b, g - 1)
                    if not tail:
                        continue
                    if g == 2:
                        evict("x1t", t1, x1t[:].rearrange("p c s -> p (c s)"))
                    if g == 3:
                        act.wait_ge(done["cq"], t1 + 1)
                        for c in range(DC):
                            act.activation(q2t[:, c, :], job_bank["cq"][:, c * S:c * S + S], ACT.Identity,
                                           bias=bq_sb[:, c:c + 1]).then_inc(freed["cq"], 1)
                    if g == 4:
                        act.wait_ge(cneg_done, t1 + 1)
                        for t in range(TB):
                            act.activation(p2[:, t, :], job_bank["cs"][:, t * LK:t * LK + LK], ACT.Exp,
                                           bias=cneg[:, t:t + 1], scale=D ** -0.5,
                                           accum_out=csum[:, t:t + 1]).then_inc(freed["cs"], 1)
                    if g == 5:
                        evict("p2t", t1, p2t[:].rearrange("k t p -> k (t p)"), job_bank["p2t"][0:LK, 0:TB * P])
                    if g == 6:
                        rstd(1, t1, mv2, lnv2)

            act.wait_ge(consts, 1)
            act.wait_ge(pro_ev, 13)
            round_(0, True, False, False)
            round_(1, True, True, False)
            with act.Fori(2, B) as b:
                round_(b, True, True, True)
            round_(B, False, True, True)
            round_(B + 1, False, False, True)

            w(act, tables, 2)

            def keys_of_pair(i, par):
                w(act, h_done, i - 1)
                for j in range(2):
                    e = act.value_load(exp_tab[0:1, bass.ds(i * 2 + j, 1)], min_val=0, max_val=NE - 1)
                    ins = act.activation(expert_keys[par][:, j, :],
                                         keys_sb[:, bass.ds(e, 1), :, :].rearrange("p a c f -> p (a c f)"), ACT.Copy)
                ins.then_inc(keys_ready, 1)

            def tiles(i, par, more=True):
                if more:
                    keys_of_pair(i + 1, (par + 1) % 2)
                act.wait_ge(h_done, i + 1)
                w(act, y_done, i - 1)
                act.activation(ht[par][:].rearrange("p j t -> p (j t)"), bank_t[par][:, 0:2 * P], ACT.Relu).then_inc(h_ready, 1)

            keys_of_pair(0, 0)
            tiles(0, 0)
            tiles(1, 1)
            with act.Fori(1, NP2 // 2 - 1) as m:
                tiles(m * 2, 0)
                tiles(m * 2 + 1, 1)
            tiles(NP2 - 2, 0)
            tiles(NP2 - 1, 1, more=False)

            for q in range(NT // QT):
                f = slice(QT * q, QT * q + QT)
                act.wait_ge(var3_done, q + 1)
                act.activation(ln3[:, 4, f], ln3[:, 3, f], ACT.Ln).then_inc(rstd3_done, 1)
                act.wait_ge(rstd3_done, 2 * q + 1)
                act.activation(ln3[:, 5, f], ln3[:, 4, f], ACT.Exp, scale=-0.5).then_inc(rstd3_done, 1)

        @block.vector
        def _(dve):
            dve.wait_ge(consts, 1)
            dve.wait_ge(weights_in, 16 * (11 + PAIRS))
            dve.wait_ge(pro_pe, 1)
            HB = B // 2
            for h in range(2):
                f = slice(h * HB * LK, (h + 1) * HB * LK)
                dve.tensor_copy(ctx_t[:, f], bank_s[h][:, 0:HB * LK]).then_inc(pro_ev, 1)
                dve.tensor_copy(ctx2_t[:, f], bank_t[h][0:TXT2, 0:HB * LK]).then_inc(pro_ev, 1)
            dve.tensor_copy(sel_t[:].rearrange("p c e -> p (c e)"), bank_o[:, 0:DC * NE]).then_inc(pro_ev, 1)
            dve.wait_ge(pro_pe, 2)
            for i in range(B // 2):
                bank = [*bank_m, bank_o][i]
                dve.tensor_tensor(out=v2[:, 2 * i:2 * i + 2, :], in0=bank[0:LK, :].rearrange("k (n d) -> k n d", n=2),
                                  in1=bv_sb[:].unsqueeze(1).broadcast_to([LK, 2, D]), op=ALU.add).then_inc(pro_ev, 1)
            dve.wait_ge(pro_pe, 3)
            for c in range(DC):
                for h in range(2):
                    dve.tensor_scalar(k2t[:, c, h * HB * LK:(h + 1) * HB * LK], [*bank_s, *bank_t][2 * c + h][:, 0:HB * LK],
                                      bk_sb[:, c:c + 1], None, ALU.add).then_inc(pro_ev, 1)

            def soft_max(b, g):
                kw = keys_of(g // DC)[1]
                n = b * NG + g
                s3 = bank_s[g % 2][:, 0:GP * kw].rearrange("p (a j) -> p a j", a=GP)
                dve.wait_ge(s_ready, n + 1)
                dve.tensor_reduce(mx[g % 2][:], s3, AX.X, ALU.max).then_inc(mx_done, 1)
                w(dve, t_done, n - 1)
                dve.wait_ge(mx_done, n + 1)
                dve.tensor_tensor(out=pb[g % 2][:, 0:GP * kw].rearrange("p (a j) -> p a j", a=GP), in0=s3,
                                  in1=mx[g % 2][:].unsqueeze(2).broadcast_to([P, GP, kw]), op=ALU.subtract)\
                    .then_inc(sub_done, 1)

            def normalise(b, g):
                qb, c = g // DC, g % DC
                n = b * NG + g
                o3 = bank_o[:, 0:GP * VC].rearrange("p (a v) -> p a v", a=GP)
                dve.wait_ge(pv_done, n + 1)
                dve.reciprocal(rs[g % 2][:], o3[:, :, 2 * DH]).then_inc(rs_done, 1)
                if g == 0:
                    w(dve, done["at"], b)
                dve.wait_ge(rs_done, n + 1)
                a3 = att[:, qb, c * GP * DH:(c + 1) * GP * DH].rearrange("p (a d) -> p a d", a=GP)
                for h in range(2):
                    q = slice(WIN * h, WIN * h + WIN)
                    dve.tensor_tensor(out=a3[q], in0=o3[q, :, h * DH:h * DH + DH],
                                      in1=rs[g % 2][q].unsqueeze(2).broadcast_to([WIN, GP, DH]), op=ALU.mult)\
                        .then_inc(norm_done, 1)

            ln1 = Steps(dve, ln1_step, TB + 4)
            ln2 = Steps(dve, ln2_step, 2 * TB + 4)
            tk = Steps(dve, topk_step, 10)
            sl = Steps(dve, slot_step, 4)

            def statistics(steps, which, r, st, mv, buf):
                for t in range(TB):
                    ins = dve.bn_stats(st[:, t, :], r[:, t, :])
                    if t == TB - 1:
                        steps.link(ins)
                    else:
                        ins.then_inc(steps.sem, 1)
                        steps.n += 1
                w(dve, steps.sem, steps.base + steps.n)
                for t in range(TB):
                    dve.bn_aggr(mv[:, t, :], st[:, t, :]).then_inc(var_done[which], 1)

            def sharpen(steps, which, t, mv, buf):
                dve.wait_ge(rstd_done[which], t + 1)
                steps.link(dve.tensor_scalar(buf[:, 0, :], mv[:, :, 1], LN_EPS, None, ALU.add))
                steps.link(dve.tensor_tensor(out=buf[:, 3, :], in0=buf[:, 2, :], in1=buf[:, 2, :], op=ALU.mult))
                steps.link(dve.scalar_tensor_tensor(out=buf[:, 4, :], in0=buf[:, 3, :], scalar=-0.5, in1=buf[:, 0, :],
                                                    op0=ALU.mult, op1=ALU.mult))
                steps.link(dve.scalar_tensor_tensor(out=buf[:, 5, :], in0=buf[:, 4, :], scalar=1.5, in1=buf[:, 2, :],
                                                    op0=ALU.add, op1=ALU.mult))

            def out_residual(t1):
                ln1.begin(t1)
                dve.wait_ge(done["op"], t1 + 1)
                dve.wait_ge(xr_in, t1 * 16 + 16)
                dve.tensor_tensor(out=r1[:].rearrange("p t d -> p (t d)"), in0=job_bank["op"][:],
                                  in1=xr[:].rearrange("p t d -> p (t d)"), op=ALU.add).then_inc(freed["op"], 1)
                dve.wait_ge(freed["op"], t1 + 1)
                statistics(ln1, 0, r1, st1, mv1, lnv)

            def layer_norm1(t1):
                sharpen(ln1, 0, t1, mv1, lnv)
                w(dve, done["x1t"], t1)
                for t in range(TB):
                    ins = dve.tensor_scalar(x1[:, t, :], r1[:, t, :], mv1[:, t, 0:1], lnv[:, 5, t:t + 1],
                                            ALU.subtract, ALU.mult)
                    ins.then_inc(x1_done, 1)
                ln1.n += 2

            def cross_max(t1):
                dve.wait_ge(done["cs"], t1 + 1)
                dve.tensor_reduce(cmx[:], job_bank["cs"][:, 0:TB * LK].rearrange("p (t k) -> p t k", t=TB), AX.X,
                                  ALU.max).then_inc(cmx_done, 1)
                dve.wait_ge(cmx_done, t1 + 1)
                dve.tensor_scalar(cneg[:], cmx[:], -(D ** -0.5), None, ALU.mult).then_inc(cneg_done, 1)

            def cross_residual(t1):
                ln2.begin(t1)
                dve.wait_ge(freed["cs"], t1 * TB + TB)
                ln2.link(dve.reciprocal(crec[:], csum[:]))
                dve.wait_ge(done["co"], t1 + 1)
                for t in range(TB):
                    ins = dve.scalar_tensor_tensor(out=r2[:, t, :], in0=job_bank["co"][:, t * D:t * D + D],
                                                   scalar=crec[:, t:t + 1], in1=x1[:, t, :], op0=ALU.mult, op1=ALU.add)
                    if t == TB - 1:
                        ins.then_inc(freed["co"], 1)
                    else:
                        ins.then_inc(ln2.sem, 1)
                        ln2.n += 1
                dve.wait_ge(freed["co"], t1 + 1)
                dve.wait_ge(ln2.sem, ln2.base + ln2.n)
                statistics(ln2, 1, r2, st2, mv2, lnv2)

            def layer_norm2(t1):
                sharpen(ln2, 1, t1, mv2, lnv2)
                w(dve, scattered, t1 * (16 * TB * TOPK))
                w(dve, x2_kept, t1 * 16)
                w(dve, done["x2t"], t1)
                for t in range(TB):
                    dve.tensor_scalar(xs[:, t, :, 0:D], r2[:, t, :].unsqueeze(1).broadcast_to([P, TOPK, D]),
                                      mv2[:, t, 0:1], lnv2[:, 5, t:t + 1], ALU.subtract, ALU.mult).then_inc(x2_done, 1)
                ln2.n += 0

            def top_experts(t2):
                tk.begin(t2)
                dve.wait_ge(freed["lg"], t2 + 1)
                tk.link(dve.tensor_scalar(ex1[:], ex[:], 1.0, None, ALU.add))
                tk.link(dve.reciprocal(gates[:], ex1[:]))
                w(dve, tk.sem, tk.base + tk.n)
                for t in range(TB):
                    ins = dve.max(top_v[:, t, :], gates[:, t, :])
                    if t == TB - 1:
                        tk.link(ins)
                    else:
                        ins.then_inc(tk.sem, 1)
                        tk.n += 1
                w(dve, tk.sem, tk.base + tk.n)
                for t in range(TB):
                    ins = dve.max_index(top_i[:, t, :], top_v[:, t, :], gates[:, t, :])
                    if t == TB - 1:
                        tk.link(ins)
                    else:
                        ins.then_inc(tk.sem, 1)
                        tk.n += 1
                tk.link(dve.tensor_copy(top_f[:], top_i[:, :, 0:TOPK]))
                tk.link(dve.tensor_tensor(out=onehot[:], in0=e_index[:],
                                          in1=top_f[:].rearrange("p t k -> p (t k)").unsqueeze(2).broadcast_to([P, TB * TOPK, NE]),
                                          op=ALU.is_equal))
                with nc.allow_low_precision("zeros and ones"):
                    dve.tensor_reduce(picked[:], onehot[:].rearrange("p (t k) e -> p t e k", t=TB), AX.X, ALU.add)\
                        .then_inc(picked_done, 1)
                dve.tensor_copy(xs[:, :, :, D + 1:D + 2], top_v[:, :, 0:TOPK].unsqueeze(3)).then_inc(tk.sem, 1)
                tk.n += 1
                tk.link(dve.tensor_copy(xs[:, :, :, D:D + 1].bitcast(I32), row_id[:].unsqueeze(3)))
                dve.tensor_scalar(row_id[:], row_id[:], S * TOPK, None, ALU.add).then_inc(row_id_done, 1)
                tk.end()

            def rows(t2):
                sl.begin(t2)
                dve.wait_ge(done["rk"], t2 + 1)
                dve.tensor_tensor(out=place[:].rearrange("p t e -> p (t e)"), in0=job_bank["rk"][:, 0:TB * NE],
                                  in1=e_start[:].rearrange("p t e -> p (t e)"), op=ALU.add).then_inc(freed["rk"], 1)
                dve.wait_ge(freed["rk"], t2 + 1)
                with nc.allow_low_precision("small whole numbers"):
                    sl.link(dve.tensor_tensor(out=so_far[:], in0=so_far[:], in1=picked[:, 0, :], op=ALU.add))
                    sl.link(dve.tensor_tensor(out=so_far[:], in0=so_far[:], in1=picked[:, 1, :], op=ALU.add))
                sl.link(dve.tensor_tensor(out=prod[:].rearrange("p (t k) e -> p t k e", t=TB),
                                          in0=onehot[:].rearrange("p (t k) e -> p t k e", t=TB),
                                          in1=place[:].unsqueeze(2).broadcast_to([P, TB, TOPK, NE]), op=ALU.mult))
                sl.link(dve.tensor_reduce(slot_f[:], prod[:], AX.X, ALU.add))
                dve.tensor_copy(slot[:], slot_f[:]).then_inc(slots_done, 1)
                sl.end()

            def round_(b, front, tail, late):
                t1, t2 = b - 1, b - 2
                if tail:
                    normalise(t1, NG - 2)
                if front:
                    dve.wait_ge(done["k"], b + 1)
                    dve.tensor_copy(kt[:].rearrange("p c s -> p (c s)"), job_bank["k"][:]).then_inc(freed["k"], 1)
                if tail:
                    normalise(t1, NG - 1)
                if late:
                    top_experts(t2)
                if front:
                    dve.wait_ge(done["v"], b + 1)
                    w(dve, vw_in, b * 32)
                    dve.tensor_copy(vw[:, 0:TB, :, 0:2 * DH],
                                    job_bank["v"][:].rearrange("p (t a v) -> p t a v", t=TB, a=PAIRS)).then_inc(freed["v"], 1)
                    soft_max(b, 0)
                if tail:
                    out_residual(t1)
                if front:
                    soft_max(b, 1)
                if tail:
                    layer_norm1(t1)
                if late:
                    rows(t2)
                for g in range(2, NG):
                    if front:
                        soft_max(b, g)
                        normalise(b, g - 2)
                    if tail and g == 4:
                        cross_max(t1)
                    if tail and g == 6:
                        cross_residual(t1)
                if tail:
                    layer_norm2(t1)

            round_(0, True, False, False)
            round_(1, True, True, False)
            with dve.Fori(2, B) as b:
                round_(b, True, True, True)
            round_(B, False, True, True)
            round_(B + 1, False, False, True)

            tb = Steps(dve, table_step, TABLE_STEPS)
            tb.begin(0)
            dve.wait_ge(counted, 1)
            counts = bank_o[:, 0:NE]
            tb.link(dve.tensor_scalar(tiles_of[:], counts, (P - 1) / 2, 1.0 / P, ALU.add, ALU.mult))
            tb.link(dve.tensor_scalar(tiles_of[:], tiles_of[:], MAGIC, None, ALU.add))
            tb.link(dve.tensor_scalar(tiles_of[:], tiles_of[:], MAGIC, None, ALU.subtract))
            tb.link(dve.tensor_tensor_scan(tiles_end[:], tiles_of[:], zeros[:], 0.0, ALU.add, ALU.add))
            tb.link(dve.tensor_scalar(ended[:], tiles_end[:], tile_no[:, 0:1], None, ALU.is_le))
            tb.link(dve.tensor_tensor(out=tiles_of[:], in0=tiles_end[:], in1=tiles_of[:], op=ALU.subtract))
            tb.link(dve.tensor_scalar(tiles_of[:], tiles_of[:], tile_no[:, 0:1], None, ALU.is_le))
            tb.link(dve.tensor_tensor(out=its_expert[:], in0=tiles_of[:], in1=ended[:], op=ALU.subtract))
            tb.link(dve.tensor_tensor(out=tile_at[:], in0=counts, in1=e_start[:, 0, :], op=ALU.add))
            tb.link(dve.scalar_tensor_tensor(out=tile_at[:], in0=tiles_end[:], scalar=-float(P), in1=tile_at[:],
                                             op0=ALU.mult, op1=ALU.add))
            tb.link(dve.scalar_tensor_tensor(out=tile_row[:], in0=tile_at[:], scalar=tile_no[:, 1:2], in1=its_expert[:],
                                             op0=ALU.add, op1=ALU.mult))
            tb.link(dve.tensor_tensor(out=tile_exp[:], in0=e_index[:, 0, :], in1=its_expert[:], op=ALU.mult))
            tb.link(dve.tensor_reduce(tile_col[:, 0:1], tile_row[:], AX.X, ALU.add))
            tb.link(dve.tensor_reduce(tile_col[:, 1:2], tile_exp[:], AX.X, ALU.add))
            tb.end()
            dve.wait_ge(turned, 1)
            dve.tensor_copy(row_tab[:], bank_s[0][0:1, 0:NTILES]).then_inc(tables, 1)
            dve.tensor_copy(exp_tab[:], bank_s[1][0:1, 0:NTILES]).then_inc(tables, 1)

            def tiles(s, k):
                u = k % 2
                if not isinstance(s, int) or s < NP2:
                    dve.wait_ge(gx_done, s + 1)
                    w(dve, h_done, s - 1)
                    dve.tensor_copy(xgt[u][:].rearrange("p j c f -> p (j c f)"), bank_s[u][:]).then_inc(gx_copied, 1)
                    dve.wait_ge(xg_in[k], (s - k) * 8 + 32)
                    w(dve, y_sent[k], (s - k) * 8)
                    dve.tensor_copy(id_gate[k][:].bitcast(I32), xg[k][:, :, D:D + 2].bitcast(I32)).then_inc(ids_kept, 1)
                if not isinstance(s, int) or s >= 2:
                    i, q = s - 2, (k - 2) % RING
                    dve.wait_ge(y_done, i + 1)
                    w(dve, ids_kept, i + 1)
                    for j in range(2):
                        ins = dve.tensor_scalar(yb[q][:, j, :], bank_m[1 + u][:, j * D:j * D + D], id_gate[q][:, j, 1:2], None,
                                                ALU.mult)
                    ins.then_inc(y_copied, 1)

            for s in range(RING):
                tiles(s, s)
            with dve.Fori(1, NP2 // RING) as m:
                for k in range(RING):
                    tiles(m * RING + k, k)
            for s in range(NP2, NP2 + 2):
                tiles(s, s % RING)

            def sums(t):
                par = t % 2
                dve.wait_ge(half_done, t + 1)
                dve.tensor_tensor(out=quarter[par][:], in0=half[par][:, 0, :], in1=half[par][:, 1, :], op=ALU.add)\
                    .then_inc(sum_step, 1)
                dve.wait_ge(sum_step, t * 2 + 1)
                dve.tensor_tensor(out=x2_all[:, t, :], in0=quarter[par][:], in1=x2_all[:, t, :], op=ALU.add).then_inc(sum_step, 1)
                dve.wait_ge(sum_step, t * 2 + 2)
                dve.bn_stats(st3[:, t, :], x2_all[:, t, :]).then_inc(stats_done, 1)

            l3 = Steps(dve, ln3_step, 8)

            def variance(q):
                f = slice(QT * q, QT * q + QT)
                l3.begin(q)
                dve.wait_ge(stats_done, QT * q + QT)
                l3.link(dve.tensor_tensor(out=ln3[:, 0, f], in0=st3[:, f, 1], in1=st3[:, f, 4], op=ALU.add))
                l3.link(dve.tensor_tensor(out=ln3[:, 1, f], in0=st3[:, f, 1], in1=st3[:, f, 4], op=ALU.subtract))
                l3.link(dve.tensor_tensor(out=ln3[:, 2, f], in0=st3[:, f, 2], in1=st3[:, f, 5], op=ALU.add))
                l3.link(dve.scalar_tensor_tensor(out=ln3[:, 1, f], in0=ln3[:, 1, f], scalar=0.25, in1=ln3[:, 1, f],
                                                 op0=ALU.mult, op1=ALU.mult))
                l3.link(dve.tensor_scalar(ln3[:, 2, f], ln3[:, 2, f], 1.0 / D, LN_EPS, ALU.mult, ALU.add))
                dve.tensor_tensor(out=ln3[:, 3, f], in0=ln3[:, 1, f], in1=ln3[:, 2, f], op=ALU.add).then_inc(var3_done, 1)

            def normalise_rows(q):
                f = slice(QT * q, QT * q + QT)
                dve.wait_ge(var3_done, q + 1)
                dve.wait_ge(rstd3_done, 2 * q + 2)
                l3.begin(q)
                l3.n = 5
                l3.link(dve.tensor_tensor(out=ln3[:, 6, f], in0=ln3[:, 5, f], in1=ln3[:, 5, f], op=ALU.mult))
                l3.link(dve.scalar_tensor_tensor(out=ln3[:, 7, f], in0=ln3[:, 6, f], scalar=-0.5, in1=ln3[:, 3, f],
                                                 op0=ALU.mult, op1=ALU.mult))
                l3.link(dve.scalar_tensor_tensor(out=ln3[:, 6, f], in0=ln3[:, 7, f], scalar=1.5, in1=ln3[:, 5, f],
                                                 op0=ALU.add, op1=ALU.mult))
                l3.end()
                dve.tensor_scalar(mean3[:, f], ln3[:, 0, f], 0.5, None, ALU.mult).then_inc(mean3_done, 1)
                dve.wait_ge(mean3_done, q + 1)
                for t in range(QT * q, QT * q + QT):
                    dve.tensor_scalar(x2_all[:, t, :], x2_all[:, t, :], mean3[:, t:t + 1], ln3[:, 6, t:t + 1],
                                      ALU.subtract, ALU.mult).then_inc(out_ready, 1)

            dve.wait_ge(x2_kept, 16 * B)
            for q in range(NT // QT):
                for t in range(QT * q, QT * q + QT):
                    sums(t)
                variance(q)
                normalise_rows(q)


_INS = ["x", "ctx_768", "L0_attn_W_qkv", "L0_attn_W_out", "L0_xattn_Wq", "L0_xattn_bq", "L0_xattn_Wk", "L0_xattn_bk",
        "L0_xattn_Wv", "L0_xattn_bv", "L0_ffn_expert_sel", "L0_ffn_keys", "L0_ffn_values"]


def kernel(**inputs):
    import numpy as np
    import concourse.bacc as bacc
    from concourse.bass_utils import run_bass_kernel_spmd as run

    nc = bacc.Bacc("TRN2", target_bir_lowering=False, num_devices=1)
    arrays, args = {}, []
    for name in _INS:
        a = np.ascontiguousarray(inputs[name])
        arrays[f"in_{name}"] = a
        args.append(nc.dram_tensor(f"in_{name}", a.shape, mybir.dt.from_np(a.dtype), kind="ExternalInput").ap())
    b, s, d = inputs["x"].shape
    n_experts = inputs["L0_ffn_expert_sel"].shape[0]
    out = nc.dram_tensor("out", (b, s, d), F32, kind="ExternalOutput").ap()
    rows = nc.dram_tensor("rows", (n_experts * (P + b * s), d + 2), F32, kind="Internal").ap()
    parts = nc.dram_tensor("parts", (b * s * 4, d), F32, kind="Internal").ap()
    decoder_layer(nc, *args, out, rows, parts)
    r = run(nc, [arrays], core_ids=[0])
    return r.results[0]["out"]
```

```python
from contextlib import ExitStack

import concourse.bass as bass
from concourse import mybir

F32 = mybir.dt.float32
BF16 = mybir.dt.bfloat16
I32 = mybir.dt.int32
U32 = mybir.dt.uint32
ALU = mybir.AluOpType
ACT = mybir.ActivationFunctionType
AX = mybir.AxisListType

P = 128
NEG = -1.0e30
MAGIC = 12582912.0
LN_EPS = 1e-5


def decoder_layer(nc, x, ctx_in, w_qkv, w_out, wq, bq, wk, bk, wv, bv, expert_sel, keys, values, out, rows_dram, parts_dram):
    B, S, D = x.shape
    LK, TXT = ctx_in.shape[1:]
    NE, _, ES = keys.shape
    TOPK, HEADS, DH, WIN = 4, 16, 16, 64
    DC = D // P
    TB = S // P
    NT = B * TB
    PAIRS = HEADS // 2
    HC = HEADS // DC
    GP = PAIRS // DC
    NQ = S // WIN
    NG = NQ * DC
    SG = 3
    VC = 2 * DH + 1
    TXT2 = TXT - P
    ROW = D + 2
    SEG = P + B * S
    NTILES = B * S * TOPK // P + NE
    NP2 = NTILES // 2
    RING = 4
    UNROLL = 2 * RING
    TABLE_STEPS = 14
    PAD_ID = 1 << 20

    with ExitStack() as stack:
        def sb(name, shape, dt=F32):
            return stack.enter_context(nc.sbuf_tensor(name, shape, dt))

        def ps(name):
            return stack.enter_context(nc.psum_tensor(name, [P, 512], F32))

        def sem(name):
            return stack.enter_context(nc.semaphore(name))

        ident = sb("ident", [P, P])
        ident_bf = sb("ident_bf", [P, P], BF16)
        mask = sb("mask", [P, GP, P], BF16)
        mask0 = sb("mask0", [P, GP, WIN], BF16)
        earlier = sb("earlier", [P, P], BF16)
        ones_bf = sb("ones_bf", [P, P], BF16)
        zeros = sb("zeros", [P, NE])
        e_index = sb("e_index", [P, TB * TOPK, NE])
        e_start = sb("e_start", [P, TB, NE])
        row_id = sb("row_id", [P, TB, TOPK], I32)
        eps_col = sb("eps_col", [P, 1])
        pad_rows = sb("pad_rows", [P, ROW])
        wqkv_sb = sb("wqkv_sb", [P, DC, 3 * D])
        wo_sb = sb("wo_sb", [P, 2, D])
        wq_sb = sb("wq_sb", [P, DC, D])
        wk_sb = sb("wk_sb", [P, D])
        wk2_sb = sb("wk2_sb", [TXT2, D])
        wv_sb = sb("wv_sb", [P, D])
        wv2_sb = sb("wv2_sb", [TXT2, D])
        bq_sb = sb("bq_sb", [P, DC])
        bk_sb = sb("bk_sb", [P, DC])
        bv_sb = sb("bv_sb", [LK, D])
        sel_rows = sb("sel_rows", [NE, D])
        sel_t = sb("sel_t", [P, DC, NE])
        keys_sb = sb("keys_sb", [P, NE, DC, ES])
        values_sb = sb("values_sb", [P, NE, D])
        ctx_sb = sb("ctx_sb", [LK, B, TXT])
        ctx_t = sb("ctx_t", [P, B * LK])
        ctx2_t = sb("ctx2_t", [TXT2, B * LK])
        k2t = sb("k2t", [P, DC, B * LK])
        v2 = sb("v2", [LK, B, D])
        xf = sb("xf", [P, TB, D])
        xr = sb("xr", [P, TB, D])
        xt = sb("xt", [P, DC, S])
        qt = sb("qt", [P, DC, S])
        qx = sb("qx", [P, DC * NQ, HC, WIN])
        kt = sb("kt", [P, DC, S])
        vw = sb("vw", [P, 3, PAIRS, VC])
        pb = [sb(f"pb{i}", [P, GP * P]) for i in range(SG)]
        pt = [sb(f"pt{i}", [P, GP * P]) for i in range(2)]
        mx = [sb(f"mx{i}", [P, GP]) for i in range(SG)]
        rs = [sb(f"rs{i}", [P, GP]) for i in range(2)]
        att = sb("att", [P, NQ, P])
        att_t = sb("att_t", [P, 2, S])
        r1 = sb("r1", [P, TB, D])
        x1 = sb("x1", [P, TB, D])
        x1t = sb("x1t", [P, DC, S])
        st1 = sb("st1", [P, TB, 6])
        mv1 = sb("mv1", [P, TB, 2])
        lnv = sb("lnv", [P, 6, TB])
        st2 = sb("st2", [P, TB, 6])
        mv2 = sb("mv2", [P, TB, 2])
        lnv2 = sb("lnv2", [P, 6, TB])
        q2t = sb("q2t", [P, DC, S])
        cmx = sb("cmx", [P, TB])
        cneg = sb("cneg", [P, TB])
        csum = sb("csum", [P, TB])
        crec = sb("crec", [P, TB])
        p2 = sb("p2", [P, TB, LK])
        p2t = sb("p2t", [LK, TB, P])
        r2 = sb("r2", [P, TB, D])
        xs = sb("xs", [P, TB, TOPK, ROW])
        x2t = sb("x2t", [P, DC, S])
        ex = sb("ex", [P, TB, NE])
        ex1 = sb("ex1", [P, TB, NE])
        gates = sb("gates", [P, TB, NE])
        top_v = sb("top_v", [P, TB, 8])
        top_i = sb("top_i", [P, TB, 8], U32)
        top_f = sb("top_f", [P, TB, TOPK])
        onehot = sb("onehot", [P, TB * TOPK, NE])
        picked = sb("picked", [P, TB, NE], BF16)
        so_far = sb("so_far", [P, NE], BF16)
        place = sb("place", [P, TB, NE])
        prod = sb("prod", [P, TB * TOPK, NE])
        slot_f = sb("slot_f", [P, TB * TOPK])
        slot = sb("slot", [P, TB * TOPK], U32)
        slot_last = sb("slot_last", [P, TB * TOPK], U32)
        x2_all = sb("x2_all", [P, NT, D])

        bank_s = [ps(f"bank_s{i}") for i in range(SG)]
        bank_t = ps("bank_t")
        bank_o = ps("bank_o")
        bank_m = [ps(f"bank_m{i}") for i in range(3)]

        JOBS = ["xt", "q", "k", "v", "at", "op", "x2t", "x1t", "lg", "cq", "rk", "cs", "p2t", "co"]
        LATE = {**{j: 0 for j in ("xt", "q", "k", "v")},
                **{j: 1 for j in ("at", "op", "x1t", "cq", "cs", "p2t", "co")},
                **{j: 2 for j in ("x2t", "lg", "rk")}}
        job_bank = {j: bank_m[n % 3] for n, j in enumerate(JOBS)}
        done = {j: sem("pe_" + j) for j in JOBS}
        freed = {j: sem("free_" + j) for j in JOBS}

        wqkv_in = [sem(f"wqkv_in{i}") for i in range(3)]
        ctx_loaded = sem("ctx_loaded")
        weights_in = sem("weights_in")
        ident_ready = sem("ident_ready")
        qx_cleared = sem("qx_cleared")
        experts_in = sem("experts_in")
        consts = sem("consts")
        chain_p = sem("chain_p")
        ln1_step = sem("ln1_step")
        ln2_step = sem("ln2_step")
        topk_step = sem("topk_step")
        slot_step = sem("slot_step")
        ln3_step = sem("ln3_step")
        stats_done = sem("stats_done")
        row_id_done = sem("row_id_done")
        cmx_done = sem("cmx_done")
        ln_done = [sem("ln1_log"), sem("ln2_log")]
        ctx_turned = sem("ctx_turned")
        ctx_kept = sem("ctx_kept")
        ctx_made = sem("ctx_made")
        ctx_added = sem("ctx_added")
        xf_in = sem("xf_in")
        xr_in = sem("xr_in")
        qx_in = [sem(f"qx_in{i}") for i in range(GP)]
        vw_in = sem("vw_in")
        s_ready = sem("s_ready")
        mx_done = sem("mx_done")
        sub_done = sem("sub_done")
        exp_done = sem("exp_done")
        t_done = sem("t_done")
        pt_done = sem("pt_done")
        pv_done = sem("pv_done")
        rs_done = sem("rs_done")
        norm_done = sem("norm_done")
        var_done = [sem("var1_done"), sem("var2_done")]
        rstd_done = [sem("rstd1_done"), sem("rstd2_done")]
        x1_done = sem("x1_done")
        x2_done = sem("x2_done")
        x2_kept = sem("x2_kept")
        cneg_done = sem("cneg_done")
        picked_done = sem("picked_done")
        slots_done = sem("slots_done")
        scattered = sem("scattered")
        pads_in = sem("pads_in")
        out_in = sem("out_in")

        def room(t, at, shape):
            flat = t[:].rearrange("p a b -> p (a b)")[:, at:at + shape[0] * shape[1]]
            return flat.rearrange("p (a b) -> p a b", a=shape[0])

        spare = qx[:].rearrange("p n h q -> p (n h q)")
        xs_last = spare[:, 0:TB * TOPK * ROW].rearrange("p (t k r) -> p t k r", t=TB, k=TOPK)

        def xs_of(b):
            return xs_last if isinstance(b, int) and b == B - 1 else xs[:]

        def slot_of(b):
            return slot_last if isinstance(b, int) and b == B - 1 else slot

        xg = [sb(f"xg{i}", [P, 2, ROW])[:] for i in range(2)] + [room(wqkv_sb, i * 2 * ROW, (2, ROW)) for i in range(2)]
        id_gate = [sb(f"id_gate{i}", [P, 2, 2]) for i in range(RING)]
        xgt = [t[:].rearrange("p a b -> p (a b)").rearrange("p (j c f) -> p j c f", j=2, c=DC) for t in (x1t, q2t)]
        expert_keys = [xt, qt]
        expert_values = [xf, xr, kt, att_t]
        ht = [sb(f"ht{i}", [P, 2, P]) for i in range(2)]
        yb = [spare[:, i * 2 * D:(i + 1) * 2 * D].rearrange("p (j d) -> p j d", j=2) for i in range(RING)]
        tiles_of = sb("tiles_of", [P, NE])
        tiles_end = sb("tiles_end", [P, NE])
        tile_at = sb("tile_at", [P, NE])
        ended = sb("ended", [P, NE])
        its_expert = sb("its_expert", [P, NE])
        tile_row = sb("tile_row", [P, NE])
        tile_exp = sb("tile_exp", [P, NE])
        tile_no = sb("tile_no", [P, 2])
        tile_col = sb("tile_col", [P, 2])
        row_tab = sb("row_tab", [1, NTILES], I32)
        exp_tab = sb("exp_tab", [1, NTILES], I32)
        counted = sem("counted")
        turned = sem("turned")
        tables = sem("tables")
        table_step = sem("table_step")
        xg_in = [sem(f"xg_in{i}") for i in range(RING)]
        ids_kept = sem("ids_kept")
        weights_ready = sem("weights_ready")
        gx_done = sem("gx_done")
        gx_copied = sem("gx_copied")
        h_done = sem("h_done")
        h_ready = sem("h_ready")
        y_done = sem("y_done")
        y_copied = sem("y_copied")
        y_sent = [sem(f"y_sent{i}") for i in range(RING)]
        PR = 4
        QT = 2
        parts_sb = [spare[:, i * TOPK * D:(i + 1) * TOPK * D].rearrange("p (k d) -> p k d", k=TOPK) for i in range(PR)]
        expert_room = keys_sb[:].rearrange("p e c f -> p (e c f)")
        half = [expert_room[:, i * 4 * D:(i + 1) * 4 * D].rearrange("p (t k d) -> p t k d", t=2, k=2) for i in range(2)]
        quarter = [x1, r1]
        st3 = sb("st3", [P, NT, 6])
        mv3 = sb("mv3", [P, NT, 2])
        ln3 = sb("ln3", [P, 7, NT])
        parts_in = [sem(f"parts_in{i}") for i in range(PR)]
        half_done = sem("half_done")
        sum_step = sem("sum_step")
        var3_done = sem("var3_done")
        rstd3_done = sem("rstd3_done")
        shift_done = sem("shift_done")
        last_ready = sem("last_ready")
        out_ready = sem("out_ready")

        passed = {}

        def w(eng, s, n):
            if not isinstance(n, int) or n > 0:
                eng.wait_ge(s, n)
            if not isinstance(n, int):
                eng.sem_inc(passed[eng_name(eng)], 1)

        def table(eng, tab, i, most):
            return nc.values_load_multi_w_load_instructions(
                tab[0:1, bass.ds(i * 2, 4)], engines=(eng.engine,), min_val=0, max_val=most,
                skip_runtime_bounds_check_because="the table's entries are in range for any counts")[1]

        def eng_name(eng):
            return str(eng.engine)

        def bank_free(eng, job, b):
            n = JOBS.index(job)
            last = JOBS[n - 3] if n >= 3 else JOBS[{0: 12, 1: 13, 2: 11}[n]]
            count = b - LATE[last] + (1 if n >= 3 else 0)
            w(eng, freed[last], min(count, B) if isinstance(b, int) else count)

        class Steps:
            def __init__(self, eng, s, per):
                self.eng, self.sem, self.per = eng, s, per

            def begin(self, b):
                self.base, self.n = b * self.per, 0

            def link(self, ins):
                self.n += 1
                ins.then_inc(self.sem, 1)
                self.eng.wait_ge(self.sem, self.base + self.n)

            def end(self):
                assert self.n == self.per, (self.n, self.per)

        def before(g):
            return {0: 2, 1: 2, 2: 5}.get(g, SG)

        def ctx_piece(i):
            return bank_m[(i + 1) % 3]

        def keys_of(qb):
            return (0, WIN) if qb == 0 else (WIN * (qb - 1), P)

        for e in (nc.tensor, nc.vector, nc.scalar, nc.gpsimd, nc.sync):
            passed[eng_name(e)] = sem("passed_" + eng_name(e).split(".")[-1])

        block = stack.enter_context(nc.Block())

        @block.sync
        def _(sp):
            def x_of(b):
                return x[bass.ds(b, 1)].rearrange("a (t p) d -> p (a t) d", p=P)

            sp.dma_start(xf[:], x_of(0)).then_inc(xf_in, 16)
            for i in range(3):
                sp.dma_start(wqkv_sb[:, :, i * D:i * D + D], w_qkv[:, i * D:i * D + D].rearrange("(c p) n -> p c n", p=P))\
                    .then_inc(wqkv_in[i], 16)
            sp.dma_start(ctx_sb[:], ctx_in.rearrange("b k t -> k b t")).then_inc(ctx_loaded, 16)
            sp.dma_start(sel_rows[:], expert_sel).then_inc(ctx_loaded, 16)

            sp.dma_start(wk_sb[:], wk[0:P, :]).then_inc(ctx_loaded, 16)
            sp.dma_start(wk2_sb[:], wk[P:TXT, :]).then_inc(ctx_loaded, 16)
            sp.dma_start(wv_sb[:], wv[0:P, :]).then_inc(ctx_loaded, 16)
            sp.dma_start(wv2_sb[:], wv[P:TXT, :]).then_inc(ctx_loaded, 16)
            sp.dma_start(bv_sb[:], bv.partition_broadcast(LK)).then_inc(ctx_loaded, 16)
            sp.dma_start(bk_sb[:], bk.rearrange("(c p) -> p c", p=P), allow_slow_non_contiguous=True).then_inc(ctx_loaded, 16)

            def load_weights():
                w_heads = w_out.rearrange("(a r d) n -> a d r n", r=2, d=DH)
                for a in range(PAIRS):
                    sp.dma_start(wo_sb[DH * a:DH * a + DH], w_heads[a]).then_inc(weights_in, 16)
                sp.dma_start(xr[:], x_of(0)).then_inc(xr_in, 16)
                sp.dma_start(wq_sb[:], wq.rearrange("(c p) n -> p c n", p=P)).then_inc(weights_in, 16)
                sp.dma_start(bq_sb[:], bq.rearrange("(c p) -> p c", p=P), allow_slow_non_contiguous=True).then_inc(weights_in, 16)

            def spread(b):
                w(sp, freed["q"], b + 1)
                w(sp, s_ready, NG * b)
                for j in range(HC):
                    sp.dma_start(qx[DH * j:DH * j + DH, :, j, :],
                                 qt[DH * j:DH * j + DH, :, :].rearrange("p c (n q) -> p (c n) q", q=WIN)).then_inc(qx_in[j // 2], 16)
                w(sp, freed["v"], b + 1)
                sp.dma_start(vw[0:WIN, 2], vw[WIN:P, 0]).then_inc(vw_in, 16)
                sp.dma_start(vw[WIN:P, 2], vw[0:WIN, 1]).then_inc(vw_in, 16)

            def next_x(b):
                w(sp, done["xt"], b)
                sp.dma_start(xf[:], x_of(b)).then_inc(xf_in, 16)

            def next_residual(b):
                w(sp, freed["op"], b)
                sp.dma_start(xr[:], x_of(b)).then_inc(xr_in, 16)

            def keep_x2(b):
                w(sp, x2_done, TB * (b + 1))
                sp.dma_start(x2_all[:, bass.ds(b * TB, TB), :], xs_of(b)[:, :, 0, 0:D]).then_inc(x2_kept, 16)

            EB = NE // B

            def experts_of(b):
                e = bass.ds(b * EB, EB)
                for c in range(DC):
                    sp.dma_start(keys_sb[:, e, c, :], keys[e, c * P:c * P + P, :].rearrange("e p f -> p e f"))\
                        .then_inc(experts_in, 16)
                sp.dma_start(values_sb[:, e, :], values[e].rearrange("e f v -> f e v")).then_inc(experts_in, 16)
                sp.dma_start(rows_dram.rearrange("(e r) d -> r e d", e=NE)[0:P, e],
                             pad_rows[:].unsqueeze(1).broadcast_to([P, EB, ROW])).then_inc(pads_in, 16)

            w(sp, qx_cleared, 1)
            spread(0)
            load_weights()
            next_x(1)
            w(sp, consts, 1)
            experts_of(0)
            next_x(2)
            spread(1)
            next_residual(1)
            experts_of(1)
            with sp.Fori(2, B - 1) as b:
                next_x(b + 1)
                spread(b)
                next_residual(b)
                keep_x2(b - 2)
                experts_of(b)
            spread(B - 1)
            keep_x2(B - 3)
            next_residual(B - 1)
            experts_of(B - 1)
            keep_x2(B - 2)
            keep_x2(B - 1)

            w(sp, pads_in, 16 * B)
            w(sp, tables, 2)
            w(sp, scattered, 16 * TB * TOPK * B)

            def rows_of(i, k, first_rows):
                w(sp, gx_done, i - RING + 1)
                w(sp, ids_kept, i - RING + 1)
                for j in range(2):
                    sp.dma_start(xg[k][:, j, :], rows_dram[bass.ds(first_rows[j], P), :]).then_inc(xg_in[k], 16)

            def rows_of_ring(i):
                for k in range(0, RING, 2):
                    r = table(sp, row_tab, i + k, NE * SEG - P)
                    rows_of(i + k, k, r[0:2])
                    rows_of(i + k + 1, k + 1, r[2:4])

            rows_of_ring(0)
            with sp.Fori(1, NP2 // RING) as m:
                rows_of_ring(m * RING)

            for k in range(RING):
                w(sp, y_sent[k], 32 * (NP2 // RING))
            parts = parts_dram.rearrange("(t p k) d -> t p k d", p=P, k=TOPK)

            def parts_of(t, k):
                w(sp, half_done, t - PR + 1)
                sp.dma_start(parts_sb[k], parts[bass.ds(t, 1)].rearrange("a p k d -> (a p) k d")).then_inc(parts_in[k], 16)

            for k in range(PR):
                parts_of(k, k)
            with sp.Fori(1, NT // PR) as m:
                for k in range(PR):
                    parts_of(m * PR + k, k)
            out_tiles = out.rearrange("b (t p) d -> p (b t) d", p=P)
            for q in range(NT // QT):
                if q < NT // QT - 1:
                    w(sp, out_ready, QT * (q + 1))
                else:
                    w(sp, last_ready, QT)
                sp.dma_start(out_tiles[:, QT * q:QT * q + QT, :], x2_all[:, QT * q:QT * q + QT, :]).then_inc(out_in, 16)
            w(sp, out_in, 16 * (NT // QT))

        @block.gpsimd
        def _(pool):
            count = [0]

            def link(ins):
                count[0] += 1
                ins.then_inc(chain_p, 1)
                w(pool, chain_p, count[0])

            link(pool.memset(ident[:], 0.0))
            pool.affine_select(out=ident[:], in_=ident[:], compare_op=ALU.not_equal, fill=1.0, base=0,
                               pattern=[[-1, P]], channel_multiplier=1).then_inc(ident_ready, 1)
            link(pool.memset(ident_bf[:], 0.0))
            link(pool.affine_select(out=ident_bf[:], in_=ident_bf[:], compare_op=ALU.not_equal, fill=1.0, base=0,
                                    pattern=[[-1, P]], channel_multiplier=1))
            link(pool.memset(vw[:, :, :, 2 * DH:VC], 1.0))
            link(pool.memset(mask[:], 0.0))
            link(pool.memset(mask0[:], 0.0))
            for h in range(2):
                q = slice(WIN * h, WIN * h + WIN)
                link(pool.affine_select(out=mask[q], in_=mask[q], compare_op=ALU.is_gt, fill=NEG, base=0,
                                        pattern=[[0, GP], [1, P]], channel_multiplier=-1))
                link(pool.affine_select(out=mask[q], in_=mask[q], compare_op=ALU.is_ge, fill=NEG, base=WIN,
                                        pattern=[[0, GP], [-1, P]], channel_multiplier=1))
                link(pool.affine_select(out=mask0[q], in_=mask0[q], compare_op=ALU.is_ge, fill=NEG, base=0,
                                        pattern=[[0, GP], [-1, WIN]], channel_multiplier=1))
            link(pool.memset(ones_bf[:], 1.0))
            link(pool.memset(earlier[:], 1.0))
            link(pool.affine_select(out=earlier[:], in_=earlier[:], compare_op=ALU.is_gt, fill=0.0, base=0,
                                    pattern=[[1, P]], channel_multiplier=-1))
            link(pool.memset(zeros[:], 0.0))
            link(pool.memset(so_far[:], 0.0))
            link(pool.memset(eps_col[:], LN_EPS))
            link(pool.iota(e_index[:], pattern=[[0, TB * TOPK], [1, NE]], base=0, channel_multiplier=0,
                           allow_small_or_imprecise_dtypes=True))
            link(pool.iota(e_start[:], pattern=[[0, TB], [SEG, NE]], base=P, channel_multiplier=0,
                           allow_small_or_imprecise_dtypes=True))
            link(pool.iota(row_id[:], pattern=[[P * TOPK, TB], [1, TOPK]], base=0, channel_multiplier=TOPK))
            link(pool.iota(tile_no[:, 0:1], pattern=[[0, 1]], base=0, channel_multiplier=1,
                           allow_small_or_imprecise_dtypes=True))
            link(pool.iota(tile_no[:, 1:2], pattern=[[0, 1]], base=0, channel_multiplier=P,
                           allow_small_or_imprecise_dtypes=True))
            link(pool.memset(pad_rows[:], 0.0))
            pool.iota(pad_rows[:, D:D + 1].bitcast(I32), pattern=[[0, 1]], base=PAD_ID, channel_multiplier=0)\
                .then_inc(consts, 1)

            def scatter(b):
                w(pool, slots_done, b + 1)
                for t in range(TB):
                    for k in range(TOPK):
                        n = t * TOPK + k
                        pool.indirect_dma_start(rows_dram, bass.IndirectOffsetOnAxis(ap=slot_of(b)[:, n:n + 1], axis=0),
                                                xs_of(b)[:, t, k, :], None).then_inc(scattered, 16)

            with pool.Fori(0, B - 1) as b:
                scatter(b)
            scatter(B - 1)

            def send(i, k):
                w(pool, y_copied, i + 1)
                for j in range(2):
                    pool.indirect_dma_start(parts_dram, bass.IndirectOffsetOnAxis(ap=id_gate[k][:, j, 0:1].bitcast(U32), axis=0),
                                            yb[k][:, j, :], None, bounds_check=B * S * TOPK - 1,
                                            oob_is_err=False).then_inc(y_sent[k], 16)

            with pool.Fori(0, NP2 // RING) as m:
                for k in range(RING):
                    send(m * RING + k, k)

            def halves(t, k, m):
                w(pool, parts_in[k], m * 16 + 16)
                w(pool, sum_step, t - k % 2 - 2)
                pool.tensor_tensor(out=half[k // 2][:, k % 2, :, :], in0=parts_sb[k][:, 0:2, :], in1=parts_sb[k][:, 2:4, :],
                                   op=ALU.add).then_inc(half_done, 1)

            for k in range(PR):
                halves(k, k, 0)
            with pool.Fori(1, NT // PR) as m:
                for k in range(PR):
                    halves(m * PR + k, k, m)

        @block.tensor
        def _(pe):
            HB = B // 2

            def turn_context():
                pe.wait_ge(ctx_loaded, 16 * 8)
                for h in range(2):
                    for i in range(HB):
                        n = h * HB + i
                        pe.transpose(bank_s[1 + h][:, i * LK:i * LK + LK], ctx_sb[:, n, 0:P], ident[0:LK, 0:LK])
                        pe.transpose([bank_t, bank_o][h][0:TXT2, i * LK:i * LK + LK], ctx_sb[:, n, P:TXT], ident[0:LK, 0:LK])
                for c in range(DC):
                    o = bank_s[1][:, HB * LK + c * NE:HB * LK + c * NE + NE]
                    last = pe.transpose(o, sel_rows[:, c * P:c * P + P], ident[0:NE, 0:NE])
                last.then_inc(ctx_turned, 1)

            def make_context(i):
                if i == 2:
                    pe.wait_ge(freed["v"], 1)
                w(pe, ctx_added, i - 2)
                bank = ctx_piece(i)
                if i < B // 2:
                    for n in range(2 * i, 2 * i + 2):
                        o = bank[0:LK, n % 2 * D:n % 2 * D + D]
                        pe.matmul(o, ctx_t[:, n * LK:n * LK + LK], wv_sb[:], start=True, stop=False)
                        last = pe.matmul(o, ctx2_t[:, n * LK:n * LK + LK], wv2_sb[:], start=False, stop=True)
                else:
                    c, h = (i - B // 2) // 2, i % 2
                    o = bank[:, 0:HB * LK]
                    f = slice(h * HB * LK, (h + 1) * HB * LK)
                    pe.matmul(o, wk_sb[:, c * P:c * P + P], ctx_t[:, f], start=True, stop=False)
                    last = pe.matmul(o, wk2_sb[:, c * P:c * P + P], ctx2_t[:, f], start=False, stop=True)
                last.then_inc(ctx_made, 1)

            def turn(job, b, src):
                bank_free(pe, job, b)
                for c in range(DC):
                    for t in range(TB):
                        o = job_bank[job][:, c * S + t * P:c * S + t * P + P]
                        last = pe.transpose(o, src(t, c), ident[:])
                last.then_inc(done[job], 1)

            def project(job, b, weights, src):
                bank_free(pe, job, b)
                for c in range(DC):
                    for k in range(DC):
                        last = pe.matmul(job_bank[job][:, c * S:c * S + S], weights(k, c), src[:, k, :],
                                         start=(k == 0), stop=(k == DC - 1))
                last.then_inc(done[job], 1)

            def project_rows(job, b, src, weights):
                bank_free(pe, job, b)
                for t in range(TB):
                    for k in range(DC):
                        last = pe.matmul(job_bank[job][:, t * D:t * D + D], src[:, k, t * P:t * P + P], weights(k),
                                         start=(k == 0), stop=(k == DC - 1))
                last.then_inc(done[job], 1)

            def score(b, g):
                qb, c = g // DC, g % DC
                k0, kw = keys_of(qb)
                n = b * NG + g
                o = bank_s[g % SG]
                w(pe, sub_done, n - before(g) + 1)
                pe.matmul(o[:, 0:GP * kw], ident_bf[:], (mask0 if qb == 0 else mask)[:].rearrange("p a j -> p (a j)"),
                          start=True, stop=False, skip_group_check=True)
                for a in range(GP):
                    if g == 0:
                        pe.wait_ge(qx_in[a], b * 32 + 32)
                    last = pe.matmul(o[:, a * kw:a * kw + kw], qx[:, c * NQ + qb, 2 * a:2 * a + 2, :].rearrange("p h q -> p (h q)"),
                                     kt[:, c, k0:k0 + kw], start=False, stop=True, skip_group_check=True)
                last.then_inc(s_ready, 1)

            def turn_probs(b, g):
                kw = keys_of(g // DC)[1]
                n = b * NG + g
                pe.wait_ge(exp_done, n + 1)
                w(pe, pt_done, n)
                for a in range(GP):
                    last = pe.transpose(bank_t[0:kw, a * P:a * P + P], pb[g % SG][:, a * kw:a * kw + kw], ident[:])
                last.then_inc(t_done, 1)

            def attend(b, g):
                qb, c = g // DC, g % DC
                kw = keys_of(qb)[1]
                n = b * NG + g
                window = [0, 0, 2, 1][qb]
                pe.wait_ge(pt_done, n + 1)
                w(pe, norm_done, 2 * n)
                if g == 0:
                    pe.wait_ge(freed["v"], b + 1)
                if g == 2 * DC:
                    pe.wait_ge(vw_in, b * 32 + 32)
                for a in range(GP):
                    last = pe.matmul(bank_o[:, a * VC:a * VC + VC], pt[g % 2][0:kw, a * P:a * P + P],
                                     vw[0:kw, window, c * GP + a, :], start=True, stop=True)
                last.then_inc(pv_done, 1)

            def round_(b, front, tail, late):
                t1, t2 = b - 1, b - 2
                first = isinstance(b, int) and b == 0
                if front:
                    pe.wait_ge(xf_in, b * 16 + 16)
                    turn("xt", b, lambda t, c: xf[:, t, c * P:c * P + P])
                if tail:
                    turn_probs(t1, NG - 2)
                    attend(t1, NG - 3)
                if front:
                    pe.wait_ge(freed["xt"], b + 1)
                    if first:
                        pe.wait_ge(wqkv_in[0], 16)
                    project("q", b, lambda k, c: wqkv_sb[:, k, c * P:c * P + P], xt)
                if tail:
                    turn_probs(t1, NG - 1)
                    attend(t1, NG - 2)
                if front:
                    if first:
                        pe.wait_ge(wqkv_in[1], 16)
                    project("k", b, lambda k, c: wqkv_sb[:, k, D + c * P:D + c * P + P], xt)
                if tail:
                    attend(t1, NG - 1)
                if front:
                    if first:
                        pe.wait_ge(wqkv_in[2], 16)
                    project_rows("v", b, xt, lambda k: wqkv_sb[:, k, 2 * D:3 * D])
                if tail:
                    bank_free(pe, "at", b)
                    pe.wait_ge(norm_done, t1 * (2 * NG) + 2 * NG)
                    for qb in range(NQ):
                        last = pe.transpose(job_bank["at"][:, qb * P:qb * P + P], att[:, qb, :], ident[:])
                    last.then_inc(done["at"], 1)
                if first:
                    turn_context()
                    pe.wait_ge(consts, 1)
                if tail:
                    pe.wait_ge(freed["at"], t1 + 1)
                    project_rows("op", b, att_t, lambda k: wo_sb[:, k, :])
                if front:
                    pe.wait_ge(freed["k"], b + 1)
                    score(b, 0)
                if first:
                    pe.wait_ge(ctx_kept, 5)
                    make_context(0)
                if front:
                    score(b, 1)
                if first:
                    make_context(1)
                if late:
                    pe.wait_ge(x2_done, t2 * TB + TB)
                    turn("x2t", b, lambda t, c: xs_of(t2)[:, t, 0, c * P:c * P + P])
                if front:
                    score(b, 2)
                    turn_probs(b, 0)
                if first:
                    make_context(2)
                for g in range(3, NG):
                    if front:
                        score(b, g)
                        turn_probs(b, g - 2)
                        attend(b, g - 3)
                    if first:
                        make_context(g)
                    if late and g == 4:
                        pe.wait_ge(freed["x2t"], t2 + 1)
                        bank_free(pe, "lg", b)
                        for t in range(TB):
                            for k in range(DC):
                                last = pe.matmul(job_bank["lg"][:, t * NE:t * NE + NE], x2t[:, k, t * P:t * P + P],
                                                 sel_t[:, k, :], start=(k == 0), stop=(k == DC - 1))
                        last.then_inc(done["lg"], 1)
                    if late and g == 5:
                        bank_free(pe, "rk", b)
                        pe.wait_ge(picked_done, t2 + 1)
                        o = job_bank["rk"]
                        pe.matmul(o[:, 0:NE], earlier[:], picked[:, 0, :], start=True, stop=False)
                        pe.matmul(o[:, 0:NE], ones_bf[:], so_far[:], start=False, stop=True)
                        pe.matmul(o[:, NE:2 * NE], earlier[:], picked[:, 1, :], start=True, stop=False)
                        pe.matmul(o[:, NE:2 * NE], ones_bf[:], picked[:, 0, :], start=False, stop=False)
                        pe.matmul(o[:, NE:2 * NE], ones_bf[:], so_far[:], start=False, stop=True).then_inc(done["rk"], 1)
                    if not tail:
                        continue
                    if g == 3:
                        pe.wait_ge(x1_done, t1 * TB + TB)
                        turn("x1t", b, lambda t, c: x1[:, t, c * P:c * P + P])
                    if g == 4:
                        pe.wait_ge(freed["x1t"], t1 + 1)
                        project("cq", b, lambda k, c: wq_sb[:, k, c * P:c * P + P], x1t)
                    if g == 5:
                        bank_free(pe, "cs", b)
                        pe.wait_ge(freed["cq"], t1 + 1)
                        for t in range(TB):
                            for k in range(DC):
                                last = pe.matmul(job_bank["cs"][:, t * LK:t * LK + LK], q2t[:, k, t * P:t * P + P],
                                                 k2t[:, k, bass.ds(t1 * LK, LK)], start=(k == 0), stop=(k == DC - 1))
                        last.then_inc(done["cs"], 1)
                    if g == 6:
                        bank_free(pe, "p2t", b)
                        w(pe, freed["cs"], t1 + 1)
                        for t in range(TB):
                            last = pe.transpose(job_bank["p2t"][0:LK, t * P:t * P + P], p2[:, t, :], ident[:])
                        last.then_inc(done["p2t"], 1)
                    if g == 7:
                        bank_free(pe, "co", b)
                        pe.wait_ge(freed["p2t"], t1 + 1)
                        for t in range(TB):
                            last = pe.matmul(job_bank["co"][:, t * D:t * D + D], p2t[:, t, :],
                                             v2[:, bass.ds(t1, 1), :].rearrange("k a d -> k (a d)"), start=True, stop=True)
                        last.then_inc(done["co"], 1)

            pe.wait_ge(ident_ready, 1)
            round_(0, True, False, False)
            pe.wait_ge(ctx_added, B)
            pe.wait_ge(weights_in, 16 * (2 + PAIRS))
            round_(1, True, True, False)
            round_(2, True, True, True)
            with pe.Fori(3, B) as b:
                round_(b, True, True, True)
            round_(B, False, True, True)
            round_(B + 1, False, False, True)

            pe.wait_ge(freed["rk"], B)
            pe.wait_ge(slot_step, 4 * B)
            pe.matmul(bank_o[:, 0:NE], ones_bf[:], so_far[:], start=True, stop=True).then_inc(counted, 1)
            pe.wait_ge(table_step, TABLE_STEPS)
            pe.transpose(bank_s[0][0:1, 0:NTILES], tile_col[0:NTILES, 0:1], ident[0:NTILES, 0:NTILES])
            pe.transpose(bank_s[1][0:1, 0:NTILES], tile_col[0:NTILES, 1:2], ident[0:NTILES, 0:NTILES]).then_inc(turned, 1)
            pe.wait_ge(tables, 2)
            pe.wait_ge(experts_in, 16 * 12)

            bank_x, bank_h, bank_y = bank_s, [bank_t, bank_m[0]], bank_m[1:]

            def tiles(s, k):
                if not isinstance(s, int) or s < NP2:
                    i, u = s, k % 2
                    pe.wait_ge(xg_in[k], (s - k) * 8 + 32)
                    w(pe, gx_copied, i - 1)
                    for j in range(2):
                        for c in range(DC):
                            last = pe.transpose(bank_x[u][:, (j * DC + c) * P:(j * DC + c) * P + P],
                                                xg[k][:, j, c * P:c * P + P], ident[:])
                    last.then_inc(gx_done, 1)
                if not isinstance(s, int) or 1 <= s <= NP2:
                    i, u = s - 1, (k + 1) % 2
                    pe.wait_ge(gx_copied, i + 1)
                    pe.wait_ge(weights_ready, i + 1)
                    w(pe, h_ready, i - 1)
                    for j in range(2):
                        for c in range(DC):
                            last = pe.matmul(bank_h[u][:, j * P:j * P + P],
                                             expert_keys[u][:].rearrange("p j (c f) -> p j c f", c=DC)[:, j, c, :],
                                             xgt[u][:, j, c, :], start=(c == 0), stop=(c == DC - 1))
                    last.then_inc(h_done, 1)
                if not isinstance(s, int) or 2 <= s <= NP2 + 1:
                    i, u = s - 2, k % 2
                    pe.wait_ge(h_ready, i + 1)
                    w(pe, y_copied, i - 1)
                    for j in range(2):
                        last = pe.matmul(bank_y[u][:, j * D:j * D + D], ht[u][:, j, :],
                                         expert_values[(k - 2) % RING][:, j, :], start=True, stop=True)
                    last.then_inc(y_done, 1)

            for s in range(UNROLL):
                tiles(s, s % RING)
            with pe.Fori(1, NP2 // UNROLL) as m:
                for k in range(UNROLL):
                    tiles(m * UNROLL + k, k % RING)
            for s in range(NP2, NP2 + 2):
                tiles(s, s % RING)

        @block.scalar
        def _(act):
            def exps(b, g):
                kw = keys_of(g // DC)[1]
                n = b * NG + g
                act.wait_ge(sub_done, n + 1)
                act.activation(pb[g % SG][:, 0:GP * kw], pb[g % SG][:, 0:GP * kw], ACT.Exp, scale=DH ** -0.5)\
                    .then_inc(exp_done, 1)

            def probs_copy(b, g):
                kw = keys_of(g // DC)[1]
                n = b * NG + g
                act.wait_ge(t_done, n + 1)
                w(act, pv_done, n - 1)
                act.activation(pt[g % 2][0:kw, :], bank_t[0:kw, :], ACT.Copy).then_inc(pt_done, 1)

            def evict(job, t, dst, src=None):
                act.wait_ge(done[job], t + 1)
                act.activation(dst, job_bank[job][:, 0:DC * S] if src is None else src, ACT.Copy).then_inc(freed[job], 1)

            def rstd(which, t, mv, buf):
                act.wait_ge(var_done[which], t * TB + TB)
                act.activation(buf[:, 1, :], mv[:, :, 1], ACT.Ln, bias=eps_col[:]).then_inc(ln_done[which], 1)
                act.wait_ge(ln_done[which], t + 1)
                act.activation(buf[:, 2, :], buf[:, 1, :], ACT.Exp, scale=-0.5).then_inc(rstd_done[which], 1)

            def round_(b, front, tail, late):
                t1, t2 = b - 1, b - 2
                if front:
                    w(act, done["v"], b)
                    evict("xt", b, xt[:].rearrange("p c s -> p (c s)"))
                if tail:
                    probs_copy(t1, NG - 2)
                if front:
                    w(act, s_ready, b * NG)
                    evict("q", b, qt[:].rearrange("p c s -> p (c s)"))
                if late:
                    rstd(1, t2, mv2, lnv2)
                if tail:
                    probs_copy(t1, NG - 1)
                    evict("at", t1, att_t[:].rearrange("p r (n i) -> p n r i", n=NQ),
                          job_bank["at"][:].rearrange("p (n r i) -> p n r i", n=NQ, r=2))
                if tail:
                    rstd(0, t1, mv1, lnv)
                if front:
                    exps(b, 0)
                if front:
                    exps(b, 1)
                if late:
                    evict("x2t", t2, x2t[:].rearrange("p c s -> p (c s)"))
                if front:
                    probs_copy(b, 0)
                    exps(b, 2)
                for g in range(3, NG):
                    if front:
                        probs_copy(b, g - 2)
                        exps(b, g)
                    if late and g == 4:
                        act.wait_ge(done["lg"], t2 + 1)
                        act.activation(ex[:].rearrange("p t e -> p (t e)"), job_bank["lg"][:, 0:TB * NE], ACT.Exp, scale=-1.0)\
                            .then_inc(freed["lg"], 1)
                    if not tail:
                        continue
                    if g == 3:
                        evict("x1t", t1, x1t[:].rearrange("p c s -> p (c s)"))
                    if g == 4:
                        act.wait_ge(done["cq"], t1 + 1)
                        for c in range(DC):
                            ins = act.activation(q2t[:, c, :], job_bank["cq"][:, c * S:c * S + S], ACT.Identity,
                                                 bias=bq_sb[:, c:c + 1])
                        ins.then_inc(freed["cq"], 1)
                    if g == 5:
                        act.wait_ge(cneg_done, t1 + 1)
                        for t in range(TB):
                            ins = act.activation(p2[:, t, :], job_bank["cs"][:, t * LK:t * LK + LK], ACT.Exp,
                                                 bias=cneg[:, t:t + 1], scale=D ** -0.5, accum_out=csum[:, t:t + 1])
                        ins.then_inc(freed["cs"], 1)
                    if g == 6:
                        evict("p2t", t1, p2t[:].rearrange("k t p -> k (t p)"), job_bank["p2t"][0:LK, 0:TB * P])

            act.preload_act_table_set("natural_log_exp_and_others")
            round_(0, True, False, False)
            act.wait_ge(weights_in, 16 * (2 + PAIRS))
            round_(1, True, True, False)
            round_(2, True, True, True)
            with act.Fori(3, B) as b:
                round_(b, True, True, True)
            round_(B, False, True, True)
            round_(B + 1, False, False, True)

            w(act, tables, 2)

            def weights_of(i, k, experts):
                w(act, h_done, i - 1)
                w(act, y_done, i - RING + 1)
                for j in range(2):
                    e = experts[j]
                    act.activation(expert_keys[k % 2][:, j, :],
                                   keys_sb[:, bass.ds(e, 1), :, :].rearrange("p a c f -> p (a c f)"), ACT.Copy)
                    ins = act.activation(expert_values[k][:, j, :],
                                         values_sb[:, bass.ds(e, 1), :].rearrange("p a v -> p (a v)"), ACT.Copy)
                ins.then_inc(weights_ready, 1)

            def weights_of_ring(i):
                for k in range(0, RING, 2):
                    e = table(act, exp_tab, i + k, NE - 1)
                    weights_of(i + k, k, e[0:2])
                    weights_of(i + k + 1, k + 1, e[2:4])

            weights_of_ring(0)
            with act.Fori(1, NP2 // RING) as m:
                weights_of_ring(m * RING)

            def last_rstd(q):
                f = slice(QT * q, QT * q + QT)
                act.wait_ge(var3_done, QT * q + QT)
                act.activation(ln3[:, 0, f], mv3[:, f, 1], ACT.Ln, bias=eps_col[:]).then_inc(rstd3_done, 1)
                act.wait_ge(rstd3_done, 2 * q + 1)
                act.activation(ln3[:, 1, f], ln3[:, 0, f], ACT.Exp, scale=-0.5).then_inc(rstd3_done, 1)

            def last_rows(q):
                act.wait_ge(shift_done, q + 1)
                for t in range(QT * q, QT * q + QT):
                    act.activation(x2_all[:, t, :], x2_all[:, t, :], ACT.Identity, scale=ln3[:, 5, t:t + 1],
                                   bias=ln3[:, 6, t:t + 1]).then_inc(out_ready, 1)

            for q in range(NT // QT):
                last_rstd(q)
                if q > 0:
                    last_rows(q - 1)

        @block.vector
        def _(dve):
            HB = B // 2
            dve.memset(qx[:], 0.0).then_inc(qx_cleared, 1)

            def keep_context():
                dve.wait_ge(ctx_turned, 1)
                for h in range(2):
                    f = slice(h * HB * LK, (h + 1) * HB * LK)
                    dve.tensor_copy(ctx_t[:, f], bank_s[1 + h][:, 0:HB * LK]).then_inc(ctx_kept, 1)
                    dve.tensor_copy(ctx2_t[:, f], [bank_t, bank_o][h][0:TXT2, 0:HB * LK]).then_inc(ctx_kept, 1)
                dve.tensor_copy(sel_t[:].rearrange("p c e -> p (c e)"), bank_s[1][:, HB * LK:HB * LK + DC * NE]).then_inc(ctx_kept, 1)
                dve.wait_ge(ctx_loaded, 16 * 8)

            def add_bias(i):
                dve.wait_ge(ctx_made, i + 1)
                bank = ctx_piece(i)
                if i < B // 2:
                    dve.tensor_tensor(out=v2[:, 2 * i:2 * i + 2, :], in0=bank[0:LK, :].rearrange("k (n d) -> k n d", n=2),
                                      in1=bv_sb[:].unsqueeze(1).broadcast_to([LK, 2, D]), op=ALU.add).then_inc(ctx_added, 1)
                else:
                    c, h = (i - B // 2) // 2, i % 2
                    dve.tensor_scalar(k2t[:, c, h * HB * LK:(h + 1) * HB * LK], bank[:, 0:HB * LK],
                                      bk_sb[:, c:c + 1], None, ALU.add).then_inc(ctx_added, 1)

            def soft_max(b, g):
                kw = keys_of(g // DC)[1]
                n = b * NG + g
                s3 = bank_s[g % SG][:, 0:GP * kw].rearrange("p (a j) -> p a j", a=GP)
                dve.wait_ge(s_ready, n + 1)
                dve.tensor_reduce(mx[g % SG][:], s3, AX.X, ALU.max).then_inc(mx_done, 1)
                w(dve, t_done, n - before(g) + 1)
                dve.wait_ge(mx_done, n + 1)
                dve.tensor_tensor(out=pb[g % SG][:, 0:GP * kw].rearrange("p (a j) -> p a j", a=GP), in0=s3,
                                  in1=mx[g % SG][:].unsqueeze(2).broadcast_to([P, GP, kw]), op=ALU.subtract)\
                    .then_inc(sub_done, 1)

            def normalise(b, g):
                qb, c = g // DC, g % DC
                n = b * NG + g
                o3 = bank_o[:, 0:GP * VC].rearrange("p (a v) -> p a v", a=GP)
                dve.wait_ge(pv_done, n + 1)
                dve.reciprocal(rs[g % 2][:], o3[:, :, 2 * DH]).then_inc(rs_done, 1)
                if g == 0:
                    w(dve, done["at"], b)
                dve.wait_ge(rs_done, n + 1)
                a3 = att[:, qb, c * GP * DH:(c + 1) * GP * DH].rearrange("p (a d) -> p a d", a=GP)
                for h in range(2):
                    q = slice(WIN * h, WIN * h + WIN)
                    dve.tensor_tensor(out=a3[q], in0=o3[q, :, h * DH:h * DH + DH],
                                      in1=rs[g % 2][q].unsqueeze(2).broadcast_to([WIN, GP, DH]), op=ALU.mult)\
                        .then_inc(norm_done, 1)

            ln1 = Steps(dve, ln1_step, TB + 3)
            ln2 = Steps(dve, ln2_step, 2 * TB + 3)
            tk = Steps(dve, topk_step, 10)
            sl = Steps(dve, slot_step, 4)

            def statistics(steps, which, r, st, mv, buf):
                for t in range(TB):
                    ins = dve.bn_stats(st[:, t, :], r[:, t, :])
                    if t == TB - 1:
                        steps.link(ins)
                    else:
                        ins.then_inc(steps.sem, 1)
                        steps.n += 1
                w(dve, steps.sem, steps.base + steps.n)
                for t in range(TB):
                    dve.bn_aggr(mv[:, t, :], st[:, t, :]).then_inc(var_done[which], 1)

            def sharpen(steps, which, t, mv, buf):
                dve.wait_ge(rstd_done[which], t + 1)
                steps.link(dve.scalar_tensor_tensor(out=buf[:, 3, :], in0=mv[:, :, 1], scalar=LN_EPS, in1=buf[:, 2, :],
                                                    op0=ALU.add, op1=ALU.mult))
                steps.link(dve.scalar_tensor_tensor(out=buf[:, 4, :], in0=buf[:, 3, :], scalar=-0.5, in1=buf[:, 2, :],
                                                    op0=ALU.mult, op1=ALU.mult))
                steps.link(dve.scalar_tensor_tensor(out=buf[:, 5, :], in0=buf[:, 4, :], scalar=1.5, in1=buf[:, 2, :],
                                                    op0=ALU.add, op1=ALU.mult))

            def out_residual(t1):
                ln1.begin(t1)
                dve.wait_ge(done["op"], t1 + 1)
                dve.wait_ge(xr_in, t1 * 16 + 16)
                dve.tensor_tensor(out=r1[:].rearrange("p t d -> p (t d)"), in0=job_bank["op"][:],
                                  in1=xr[:].rearrange("p t d -> p (t d)"), op=ALU.add).then_inc(freed["op"], 1)
                dve.wait_ge(freed["op"], t1 + 1)
                statistics(ln1, 0, r1, st1, mv1, lnv)

            def layer_norm1(t1):
                sharpen(ln1, 0, t1, mv1, lnv)
                w(dve, done["x1t"], t1)
                for t in range(TB):
                    ins = dve.tensor_scalar(x1[:, t, :], r1[:, t, :], mv1[:, t, 0:1], lnv[:, 5, t:t + 1],
                                            ALU.subtract, ALU.mult)
                    ins.then_inc(x1_done, 1)
                ln1.n += 2

            def cross_max(t1):
                dve.wait_ge(done["cs"], t1 + 1)
                dve.tensor_reduce(cmx[:], job_bank["cs"][:, 0:TB * LK].rearrange("p (t k) -> p t k", t=TB), AX.X,
                                  ALU.max).then_inc(cmx_done, 1)
                dve.wait_ge(cmx_done, t1 + 1)
                dve.tensor_scalar(cneg[:], cmx[:], -(D ** -0.5), None, ALU.mult).then_inc(cneg_done, 1)

            def cross_residual(t1):
                ln2.begin(t1)
                dve.wait_ge(freed["cs"], t1 + 1)
                ln2.link(dve.reciprocal(crec[:], csum[:]))
                dve.wait_ge(done["co"], t1 + 1)
                for t in range(TB):
                    ins = dve.scalar_tensor_tensor(out=r2[:, t, :], in0=job_bank["co"][:, t * D:t * D + D],
                                                   scalar=crec[:, t:t + 1], in1=x1[:, t, :], op0=ALU.mult, op1=ALU.add)
                    if t == TB - 1:
                        ins.then_inc(freed["co"], 1)
                    else:
                        ins.then_inc(ln2.sem, 1)
                        ln2.n += 1
                dve.wait_ge(freed["co"], t1 + 1)
                dve.wait_ge(ln2.sem, ln2.base + ln2.n)
                statistics(ln2, 1, r2, st2, mv2, lnv2)

            def layer_norm2(t2):
                ln2.begin(t2)
                ln2.n = 2 * TB
                sharpen(ln2, 1, t2, mv2, lnv2)
                ln2.end()
                if not isinstance(t2, int) or t2 < B - 1:
                    w(dve, scattered, t2 * (16 * TB * TOPK))
                    w(dve, x2_kept, t2 * 16)
                    w(dve, done["x2t"], t2)
                for t in range(TB):
                    dve.tensor_scalar(xs_of(t2)[:, t, :, 0:D], r2[:, t, :].unsqueeze(1).broadcast_to([P, TOPK, D]),
                                      mv2[:, t, 0:1], lnv2[:, 5, t:t + 1], ALU.subtract, ALU.mult).then_inc(x2_done, 1)

            def top_experts(t2):
                tk.begin(t2)
                dve.wait_ge(freed["lg"], t2 + 1)
                tk.link(dve.tensor_scalar(ex1[:], ex[:], 1.0, None, ALU.add))
                tk.link(dve.reciprocal(gates[:], ex1[:]))
                w(dve, tk.sem, tk.base + tk.n)
                for t in range(TB):
                    ins = dve.max(top_v[:, t, :], gates[:, t, :])
                    if t == TB - 1:
                        tk.link(ins)
                    else:
                        ins.then_inc(tk.sem, 1)
                        tk.n += 1
                w(dve, tk.sem, tk.base + tk.n)
                for t in range(TB):
                    ins = dve.max_index(top_i[:, t, :], top_v[:, t, :], gates[:, t, :])
                    if t == TB - 1:
                        tk.link(ins)
                    else:
                        ins.then_inc(tk.sem, 1)
                        tk.n += 1
                tk.link(dve.tensor_copy(top_f[:], top_i[:, :, 0:TOPK]))
                tk.link(dve.tensor_tensor(out=onehot[:], in0=e_index[:],
                                          in1=top_f[:].rearrange("p t k -> p (t k)").unsqueeze(2).broadcast_to([P, TB * TOPK, NE]),
                                          op=ALU.is_equal))
                with nc.allow_low_precision("zeros and ones"):
                    dve.tensor_reduce(picked[:], onehot[:].rearrange("p (t k) e -> p t e k", t=TB), AX.X, ALU.add)\
                        .then_inc(picked_done, 1)
                dve.tensor_copy(xs_of(t2)[:, :, :, D + 1:D + 2], top_v[:, :, 0:TOPK].unsqueeze(3)).then_inc(tk.sem, 1)
                tk.n += 1
                tk.link(dve.tensor_copy(xs_of(t2)[:, :, :, D:D + 1].bitcast(I32), row_id[:].unsqueeze(3)))
                dve.tensor_scalar(row_id[:], row_id[:], S * TOPK, None, ALU.add).then_inc(row_id_done, 1)
                tk.end()

            def rows(t2):
                sl.begin(t2)
                dve.wait_ge(done["rk"], t2 + 1)
                dve.tensor_tensor(out=place[:].rearrange("p t e -> p (t e)"), in0=job_bank["rk"][:, 0:TB * NE],
                                  in1=e_start[:].rearrange("p t e -> p (t e)"), op=ALU.add).then_inc(freed["rk"], 1)
                dve.wait_ge(freed["rk"], t2 + 1)
                sl.link(dve.tensor_tensor(out=prod[:].rearrange("p (t k) e -> p t k e", t=TB),
                                          in0=onehot[:].rearrange("p (t k) e -> p t k e", t=TB),
                                          in1=place[:].unsqueeze(2).broadcast_to([P, TB, TOPK, NE]), op=ALU.mult))
                sl.link(dve.tensor_reduce(slot_f[:], prod[:], AX.X, ALU.add))
                dve.tensor_copy(slot_of(t2)[:], slot_f[:]).then_inc(slots_done, 1)
                with nc.allow_low_precision("small whole numbers"):
                    sl.link(dve.tensor_tensor(out=so_far[:], in0=so_far[:], in1=picked[:, 0, :], op=ALU.add))
                    sl.link(dve.tensor_tensor(out=so_far[:], in0=so_far[:], in1=picked[:, 1, :], op=ALU.add))
                sl.end()

            def round_(b, front, tail, late):
                t1, t2 = b - 1, b - 2
                first = isinstance(b, int) and b == 0
                if tail:
                    normalise(t1, NG - 3)
                    normalise(t1, NG - 2)
                if front:
                    dve.wait_ge(done["k"], b + 1)
                    dve.tensor_copy(kt[:].rearrange("p c s -> p (c s)"), job_bank["k"][:]).then_inc(freed["k"], 1)
                if tail:
                    normalise(t1, NG - 1)
                if front:
                    if first:
                        dve.wait_ge(consts, 1)
                    dve.wait_ge(done["v"], b + 1)
                    w(dve, vw_in, b * 32)
                    dve.tensor_copy(vw[:, 0:TB, :, 0:2 * DH],
                                    job_bank["v"][:].rearrange("p (t a v) -> p t a v", t=TB, a=PAIRS)).then_inc(freed["v"], 1)
                if first:
                    keep_context()
                if late:
                    layer_norm2(t2)
                if tail:
                    out_residual(t1)
                if front:
                    soft_max(b, 0)
                if first:
                    add_bias(0)
                if front:
                    soft_max(b, 1)
                if first:
                    add_bias(1)
                if front:
                    soft_max(b, 2)
                if tail:
                    layer_norm1(t1)
                if first:
                    add_bias(2)
                for g in range(3, NG):
                    if front:
                        soft_max(b, g)
                        normalise(b, g - 3)
                    if first:
                        add_bias(g)
                    if late and g == 4:
                        top_experts(t2)
                    if late and g == 6:
                        rows(t2)
                    if tail and g == 5:
                        cross_max(t1)
                    if tail and g == 7:
                        cross_residual(t1)

            round_(0, True, False, False)
            round_(1, True, True, False)
            round_(2, True, True, True)
            with dve.Fori(3, B) as b:
                round_(b, True, True, True)
            round_(B, False, True, True)
            round_(B + 1, False, False, True)

            tb = Steps(dve, table_step, TABLE_STEPS)
            tb.begin(0)
            dve.wait_ge(counted, 1)
            counts = bank_o[:, 0:NE]
            tb.link(dve.tensor_scalar(tiles_of[:], counts, (P - 1) / 2, 1.0 / P, ALU.add, ALU.mult))
            tb.link(dve.tensor_scalar(tiles_of[:], tiles_of[:], MAGIC, None, ALU.add))
            tb.link(dve.tensor_scalar(tiles_of[:], tiles_of[:], MAGIC, None, ALU.subtract))
            tb.link(dve.tensor_tensor_scan(tiles_end[:], tiles_of[:], zeros[:], 0.0, ALU.add, ALU.add))
            tb.link(dve.tensor_scalar(ended[:], tiles_end[:], tile_no[:, 0:1], None, ALU.is_le))
            tb.link(dve.tensor_tensor(out=tiles_of[:], in0=tiles_end[:], in1=tiles_of[:], op=ALU.subtract))
            tb.link(dve.tensor_scalar(tiles_of[:], tiles_of[:], tile_no[:, 0:1], None, ALU.is_le))
            tb.link(dve.tensor_tensor(out=its_expert[:], in0=tiles_of[:], in1=ended[:], op=ALU.subtract))
            tb.link(dve.tensor_tensor(out=tile_at[:], in0=counts, in1=e_start[:, 0, :], op=ALU.add))
            tb.link(dve.scalar_tensor_tensor(out=tile_at[:], in0=tiles_end[:], scalar=-float(P), in1=tile_at[:],
                                             op0=ALU.mult, op1=ALU.add))
            tb.link(dve.scalar_tensor_tensor(out=tile_row[:], in0=tile_at[:], scalar=tile_no[:, 1:2], in1=its_expert[:],
                                             op0=ALU.add, op1=ALU.mult))
            tb.link(dve.tensor_tensor(out=tile_exp[:], in0=e_index[:, 0, :], in1=its_expert[:], op=ALU.mult))
            tb.link(dve.tensor_reduce(tile_col[:, 0:1], tile_row[:], AX.X, ALU.add))
            tb.link(dve.tensor_reduce(tile_col[:, 1:2], tile_exp[:], AX.X, ALU.add))
            tb.end()
            dve.wait_ge(turned, 1)
            dve.tensor_copy(row_tab[:], bank_s[0][0:1, 0:NTILES]).then_inc(tables, 1)
            dve.tensor_copy(exp_tab[:], bank_s[1][0:1, 0:NTILES]).then_inc(tables, 1)

            def tiles(s, k):
                u = k % 2
                if not isinstance(s, int) or s < NP2:
                    dve.wait_ge(gx_done, s + 1)
                    w(dve, h_done, s - 1)
                    dve.tensor_copy(xgt[u].rearrange("p j c f -> p (j c f)"), bank_s[u][:]).then_inc(gx_copied, 1)
                if not isinstance(s, int) or 1 <= s <= NP2:
                    i, u = s - 1, (k + 1) % 2
                    dve.wait_ge(h_done, i + 1)
                    w(dve, y_done, i - 1)
                    dve.tensor_scalar(ht[u][:].rearrange("p j t -> p (j t)"), [bank_t, bank_m[0]][u][:, 0:2 * P], 0.0, None,
                                      ALU.max).then_inc(h_ready, 1)
                if not isinstance(s, int) or s >= 2:
                    i, q = s - 2, (k - 2) % RING
                    dve.wait_ge(y_done, i + 1)
                    w(dve, ids_kept, i + 1)
                    for j in range(2):
                        ins = dve.tensor_scalar(yb[q][:, j, :], bank_m[1 + k % 2][:, j * D:j * D + D], id_gate[q][:, j, 1:2], None,
                                                ALU.mult)
                    ins.then_inc(y_copied, 1)
                if not isinstance(s, int) or s < NP2:
                    dve.wait_ge(xg_in[k], (s - k) * 8 + 32)
                    w(dve, y_sent[k], (s - k) * 8)
                    dve.tensor_copy(id_gate[k][:].bitcast(I32), xg[k][:, :, D:D + 2].bitcast(I32)).then_inc(ids_kept, 1)

            for s in range(UNROLL):
                tiles(s, s % RING)
            with dve.Fori(1, NP2 // UNROLL) as m:
                for k in range(UNROLL):
                    tiles(m * UNROLL + k, k % RING)
            for s in range(NP2, NP2 + 2):
                tiles(s, s % RING)

            l3 = Steps(dve, ln3_step, 3)

            def sums(t):
                par = t // 2 % 2
                dve.wait_ge(half_done, t + 2)
                dve.tensor_tensor(out=quarter[par][:], in0=half[par][:, :, 0, :], in1=half[par][:, :, 1, :], op=ALU.add)\
                    .then_inc(sum_step, 1)
                dve.wait_ge(sum_step, t + 1)
                dve.tensor_tensor(out=x2_all[:, t:t + 2, :], in0=quarter[par][:], in1=x2_all[:, t:t + 2, :], op=ALU.add)\
                    .then_inc(sum_step, 1)
                dve.wait_ge(sum_step, t + 2)
                for i in range(t, t + 2):
                    dve.bn_stats(st3[:, i, :], x2_all[:, i, :]).then_inc(stats_done, 1)

            def variance(q):
                dve.wait_ge(stats_done, QT * q + QT)
                for t in range(QT * q, QT * q + QT):
                    dve.bn_aggr(mv3[:, t, :], st3[:, t, :]).then_inc(var3_done, 1)

            def scale_and_shift(q):
                f = slice(QT * q, QT * q + QT)
                l3.begin(q)
                dve.wait_ge(var3_done, QT * q + QT)
                dve.wait_ge(rstd3_done, 2 * q + 2)
                l3.link(dve.scalar_tensor_tensor(out=ln3[:, 3, f], in0=mv3[:, f, 1], scalar=LN_EPS, in1=ln3[:, 1, f],
                                                 op0=ALU.add, op1=ALU.mult))
                l3.link(dve.scalar_tensor_tensor(out=ln3[:, 4, f], in0=ln3[:, 3, f], scalar=-0.5, in1=ln3[:, 1, f],
                                                 op0=ALU.mult, op1=ALU.mult))
                l3.link(dve.scalar_tensor_tensor(out=ln3[:, 5, f], in0=ln3[:, 4, f], scalar=1.5, in1=ln3[:, 1, f],
                                                 op0=ALU.add, op1=ALU.mult))
                l3.end()
                dve.scalar_tensor_tensor(out=ln3[:, 6, f], in0=mv3[:, f, 0], scalar=-1.0, in1=ln3[:, 5, f],
                                         op0=ALU.mult, op1=ALU.mult).then_inc(shift_done, 1)

            dve.wait_ge(x2_kept, 16 * B)
            for q in range(NT // QT):
                for t in range(QT * q, QT * q + QT, 2):
                    sums(t)
                variance(q)
                if q > 0:
                    scale_and_shift(q - 1)
            scale_and_shift(NT // QT - 1)
            dve.wait_ge(shift_done, NT // QT)
            for t in range(NT - QT, NT):
                dve.tensor_scalar(x2_all[:, t, :], x2_all[:, t, :], ln3[:, 5, t:t + 1], ln3[:, 6, t:t + 1],
                                  ALU.mult, ALU.add).then_inc(last_ready, 1)


_INS = ["x", "ctx_768", "L0_attn_W_qkv", "L0_attn_W_out", "L0_xattn_Wq", "L0_xattn_bq", "L0_xattn_Wk", "L0_xattn_bk",
        "L0_xattn_Wv", "L0_xattn_bv", "L0_ffn_expert_sel", "L0_ffn_keys", "L0_ffn_values"]


def kernel(**inputs):
    import numpy as np
    import concourse.bacc as bacc
    from concourse.bass_utils import run_bass_kernel_spmd as run

    nc = bacc.Bacc("TRN2", target_bir_lowering=False, num_devices=1)
    arrays, args = {}, []
    for name in _INS:
        a = np.ascontiguousarray(inputs[name])
        arrays[f"in_{name}"] = a
        args.append(nc.dram_tensor(f"in_{name}", a.shape, mybir.dt.from_np(a.dtype), kind="ExternalInput").ap())
    b, s, d = inputs["x"].shape
    n_experts = inputs["L0_ffn_expert_sel"].shape[0]
    out = nc.dram_tensor("out", (b, s, d), F32, kind="ExternalOutput").ap()
    rows = nc.dram_tensor("rows", (n_experts * (P + b * s), d + 2), F32, kind="Internal").ap()
    parts = nc.dram_tensor("parts", (b * s * 4, d), F32, kind="Internal").ap()
    decoder_layer(nc, *args, out, rows, parts)
    r = run(nc, [arrays], core_ids=[0])
    return r.results[0]["out"]
```
